# Optimizing a Trainium2 kernel written in Bass

```python
import numpy as np
import jax
import jax.numpy as jnp

def _softmax(x, axis=-1):
    return jax.nn.softmax(x, axis=axis)

def _gelu(x):
    return jax.nn.gelu(x, approximate=True)

def _silu(x):
    return jax.nn.silu(x)

def _sigmoid(x):
    return jax.nn.sigmoid(x)

def _layernorm(x, axis=-1, eps=1e-05):
    m = jnp.mean(x, axis=axis, keepdims=True)
    v = jnp.var(x, axis=axis, keepdims=True)
    return (x - m) / jnp.sqrt(v + eps)

def _scatter_add(tgt, idx, src, axis=0):
    return tgt.at[idx].add(src)

def _segment_sum(src, seg, n):
    return jax.ops.segment_sum(src, seg, n)
kernel_name = 'mk_xattn_ffn_d1_seqx_r8_fb1ef3'

def setup_inputs(seed: int=0):
    np.random.seed(seed)
    _w = jnp.asarray

    def _rec_inputs():
        import jax
        import jax.numpy as jnp
        _rk = jax.random.key(seed)
        x = -0.0002928 + 1 * jax.random.normal(jax.random.fold_in(_rk, 1), (16, 128, 128), jnp.float32)
        _lenS = 128 - jax.random.randint(jax.random.fold_in(_rk, 7), (16,), 0, max(1, 128 // 4) + 1, jnp.int32)
        _lenS2 = 128 - jax.random.randint(jax.random.fold_in(_rk, 8), (16,), 0, max(1, 128 // 4) + 1, jnp.int32)
        _ctx_1024P = jax.random.normal(jax.random.fold_in(_rk, 11), (16, 16, 128), jnp.float32)
        _ctx_1024c = jax.random.dirichlet(jax.random.fold_in(_rk, 511), 0.3 * jnp.ones((16,), jnp.float32), (16, 128))
        _ctx_1024t = jnp.einsum('bsk,bkd->bsd', _ctx_1024c, _ctx_1024P)
        _ctx_1024t = _ctx_1024t * jax.lax.rsqrt(jnp.mean(jnp.square(_ctx_1024t)) + 1e-12) * 0.953939
        ctx_1024 = -1.39393e-06 + 0.999914 * (_ctx_1024t + 0.3 * jax.random.normal(jax.random.fold_in(_rk, 611), (16, 128, 128), jnp.float32))
        _validS = jnp.arange(128)[None, :] < _lenS[:, None]
        _validS2 = jnp.arange(128)[None, :] < _lenS2[:, None]
        _causal = jnp.tril(jnp.ones((128, 128), dtype=bool))
        mask_BxS2_if1 = jnp.where(jnp.ones((16, 128), dtype=bool), 1, 0).astype(jnp.int32)
        return (x, ctx_1024, mask_BxS2_if1)
    x, ctx_1024, mask_BxS2_if1 = _rec_inputs()

    def _L0_xattn_setup():
        import jax, jax.numpy as jnp
        import numpy as np
        D_MODEL = 128
        NUM_HEADS = 16
        HEAD_DIM = D_MODEL // NUM_HEADS
        MASK_FUTURE = False
        NEG_INF = -1000000000.0

        def _split_heads(x):
            B, L, _ = x.shape
            return x.reshape(B, L, NUM_HEADS, HEAD_DIM).transpose(0, 2, 1, 3)
        key = jax.random.key(seed)
        ks = jax.random.split(key, 8)
        B, L = (2, 256)
        q = jax.random.normal(ks[0], (B, L, D_MODEL), dtype=jnp.float32)
        k = jax.random.normal(ks[1], (B, L, D_MODEL), dtype=jnp.float32)
        v = jax.random.normal(ks[2], (B, L, D_MODEL), dtype=jnp.float32)
        attention_mask = jnp.ones((B, L), dtype=jnp.int32)
        s = 1.0 / np.sqrt(D_MODEL)
        Wq = jax.random.normal(ks[3], (D_MODEL, D_MODEL), dtype=jnp.float32) * s
        Wk = jax.random.normal(ks[4], (D_MODEL, D_MODEL), dtype=jnp.float32) * s
        Wv = jax.random.normal(ks[5], (D_MODEL, D_MODEL), dtype=jnp.float32) * s
        Wo = jax.random.normal(ks[6], (D_MODEL, D_MODEL), dtype=jnp.float32) * s
        return {'q': q, 'k': k, 'v': v, 'attention_mask': attention_mask, 'Wq': Wq, 'Wk': Wk, 'Wv': Wv, 'Wo': Wo}
    _L0_xattn_all = _L0_xattn_setup()
    _L0_xattn_in = {k: v for k, v in _L0_xattn_all.items() if k in ('Wq', 'Wk', 'Wv', 'Wo')}
    del _L0_xattn_all

    def _L0_ffn_setup():
        import jax, jax.numpy as jnp
        import numpy as np
        TOP_K = 2
        key = jax.random.key(seed)
        k0, k1, k2, k3, k4 = jax.random.split(key, 5)
        B, S, H, I, E = (1, 512, 128, 256, 8)
        hidden_states = jax.random.normal(k0, (B, S, H), dtype=jnp.float32)
        wg = jax.random.normal(k1, (E, H), dtype=jnp.float32) * 0.02
        w1 = jax.random.normal(k2, (E, I, H), dtype=jnp.float32) * 0.02
        w3 = jax.random.normal(k3, (E, I, H), dtype=jnp.float32) * 0.02
        w2 = jax.random.normal(k4, (E, H, I), dtype=jnp.float32) * 0.02
        return {'hidden_states': hidden_states, 'wg': wg, 'w1': w1, 'w3': w3, 'w2': w2}
    _L0_ffn_all = _L0_ffn_setup()
    _L0_ffn_in = {k: v for k, v in _L0_ffn_all.items() if k in ('wg', 'w1', 'w3', 'w2')}
    del _L0_ffn_all
    return {'x': x, 'ctx_1024': ctx_1024, 'mask_BxS2_if1': mask_BxS2_if1, 'L0_xattn_Wq': _L0_xattn_in['Wq'], 'L0_xattn_Wk': _L0_xattn_in['Wk'], 'L0_xattn_Wv': _L0_xattn_in['Wv'], 'L0_xattn_Wo': _L0_xattn_in['Wo'], 'L0_ffn_wg': _L0_ffn_in['wg'], 'L0_ffn_w1': _L0_ffn_in['w1'], 'L0_ffn_w3': _L0_ffn_in['w3'], 'L0_ffn_w2': _L0_ffn_in['w2']}

def reference(x, ctx_1024, mask_BxS2_if1, L0_xattn_Wq, L0_xattn_Wk, L0_xattn_Wv, L0_xattn_Wo, L0_ffn_wg, L0_ffn_w1, L0_ffn_w3, L0_ffn_w2):
    import jax
    import jax.numpy as jnp

    def _L0_xattn_ref(q, k, v, attention_mask, Wq, Wk, Wv, Wo):
        import jax, jax.numpy as jnp
        import numpy as np
        D_MODEL = 128
        NUM_HEADS = 16
        HEAD_DIM = D_MODEL // NUM_HEADS
        MASK_FUTURE = False
        NEG_INF = -1000000000.0

        def _split_heads(x):
            B, L, _ = x.shape
            return x.reshape(B, L, NUM_HEADS, HEAD_DIM).transpose(0, 2, 1, 3)
        B, Lq, _ = q.shape
        Lk = k.shape[1]
        Q = _split_heads(q @ Wq.T)
        K = _split_heads(k @ Wk.T)
        V = _split_heads(v @ Wv.T)
        scale = HEAD_DIM ** 0.5
        scores = jnp.einsum('bhqd,bhkd->bhqk', Q, K) / scale
        mask = (attention_mask == 0)[:, None, None, :]
        scores = jnp.where(mask, NEG_INF, scores)
        if MASK_FUTURE:
            fut = jnp.triu(jnp.ones((Lq, Lk), dtype=bool), k=1)
            scores = jnp.where(fut[None, None], NEG_INF, scores)
        attn = jax.nn.softmax(scores, axis=-1)
        out = jnp.einsum('bhqk,bhkd->bhqd', attn, V)
        out = out.transpose(0, 2, 1, 3).reshape(B, Lq, D_MODEL)
        return out @ Wo.T

    def _L0_ffn_ref(hidden_states, wg, w1, w3, w2):
        import jax, jax.numpy as jnp
        import numpy as np
        TOP_K = 2
        orig_shape = hidden_states.shape
        H = orig_shape[-1]
        E = wg.shape[0]
        x = hidden_states.reshape(-1, H)
        router_logits = x @ wg.T
        probs = jax.nn.softmax(router_logits, axis=-1)
        topk_w, topk_idx = jax.lax.top_k(probs, TOP_K)
        topk_w = topk_w / jnp.sum(topk_w, axis=-1, keepdims=True)
        expert_w = jnp.sum(jax.nn.one_hot(topk_idx, E, dtype=x.dtype) * topk_w[..., None], axis=1)
        h1 = jnp.einsum('th,eih->tei', x, w1)
        h3 = jnp.einsum('th,eih->tei', x, w3)
        y = jnp.einsum('tei,ehi->teh', jax.nn.silu(h1) * h3, w2)
        out = jnp.einsum('te,teh->th', expert_w, y)
        return out.reshape(orig_shape)
    x = x + _L0_xattn_ref(_layernorm(x, axis=-1), ctx_1024, ctx_1024, mask_BxS2_if1, L0_xattn_Wq, L0_xattn_Wk, L0_xattn_Wv, L0_xattn_Wo)
    x = x + _L0_ffn_ref(_layernorm(x, axis=-1), L0_ffn_wg, L0_ffn_w1, L0_ffn_w3, L0_ffn_w2)
    return x

_drawn_inputs = setup_inputs


def setup_inputs(seed=0):
    import zlib

    import numpy as np

    out = dict(_drawn_inputs(seed))
    spreads = {}
    factors = {'L0_ffn_wg': 8.0, 'L0_ffn_w1': 8.0, 'L0_ffn_w3': 8.0, 'L0_ffn_w2': 8.0}
    for name, (base, spread) in spreads.items():
        noise = np.random.default_rng([zlib.crc32(name.encode()), seed]).standard_normal(out[name].shape)
        drawn = base * np.exp(spread * noise) if base else spread * noise
        out[name] = jnp.asarray(drawn.astype(out[name].dtype))
    for name, factor in factors.items():
        out[name] = (out[name] * factor).astype(out[name].dtype)
    return out
```

```python
from contextlib import ExitStack

import numpy as np

import concourse.bass as bass
from concourse import mybir

F32 = mybir.dt.float32
F32R = mybir.dt.float32r
I32 = mybir.dt.int32
ALU = mybir.AluOpType
ACT = mybir.ActivationFunctionType
X = mybir.AxisListType.X

P = 128
B, S, D = 16, 128, 128
H, HD = 16, 8
NG, NJ = 4, 4
R = 32
QB = 4
NQ = B // QB
T = QB * S
E, I = 8, 256
NB = E * I // P
SCALE = float(HD) ** -0.5
NEG = -1.0e9 / SCALE
EPS = 1e-5
LAG = 3
RH = 4


def split_constant(v):
    bits = np.float32(v).view(np.uint32)
    hi = np.uint32(bits & np.uint32(0xFFFFF000)).view(np.float32)
    return float(hi), float(np.float32(np.float32(v) - hi))


C_ID, C_CQ, C_CK, C_ONE, C_HEAD, C_BATCH, C_EXP, C_LOW, C_BIAS, C_N = 0, 128, 129, 130, 132, 148, 152, 160, 224, 352


def constants():
    c = np.zeros((P, C_N), np.float32)
    p = np.arange(P)
    r = p % R
    c[:, C_ID:C_ID + P] = np.eye(P)
    c[:, C_CQ] = np.where((r >= 16) & (r < 24), -1.0, np.where((r == 24) | (r == 25), 1.0, 0.0))
    c[:, C_CK] = np.where((r >= 8) & (r < 16), -1.0, 0.0)
    c[:, C_ONE] = (r == 24) | (r == 25)
    for h in range(H):
        c[:, C_HEAD + h] = p % H == h
    for b in range(QB):
        c[:, C_BATCH + b] = (p // H) % QB == b
    for e in range(E):
        c[:, C_EXP + e] = (p < 2 * E) & (p % E == e)
        c[:, C_LOW + E * e:C_LOW + E * e + e] = 1.0
    hi, lo = split_constant(NEG)
    for j in range(NJ):
        c[0, C_BIAS + R * j + 24] = hi
        c[0, C_BIAS + R * j + 25] = lo
    return c


def slot_order():
    order = ["w", "wo"]
    for u in range(NQ):
        order += [("cT", u), ("xT", u)]
        if u:
            order += [("MT", u - 1)]
        order += [("V", u)] + [("st", u, k) for k in range(2 * NG)]
    order += [("MT", NQ - 1)]
    order += [("W", k) for k in range(3 * NB // 4)]
    order += [("x2T", 0), ("lg", 0), ("ewT", 0)]
    for q in range(NQ):
        if q:
            order += [("yT", q - 1)]
        if q + 1 < NQ:
            order += [("x2T", q + 1), ("lg", q + 1), ("ewT", q + 1)]
    order += [("yT", NQ - 1)]
    return {name: n for n, name in enumerate(order)}


STACKS = [(0, 0), (0, 1), (1, 0), (1, 1), (1, 2), (1, 3), (0, 2), (0, 3)]
K_STACKS, Q_STACKS = 6, 8


def program(nc, x, ctx_in, mask, Wq, Wk, Wv, Wo, wg, w1, w3, w2, consts, out):
    slot = slot_order()
    with ExitStack() as stack:
        def sb(name, shape, dt=F32):
            return stack.enter_context(nc.sbuf_tensor(name, shape, dt))

        def sem(name):
            return stack.enter_context(nc.semaphore(name))

        cst = sb("cst", [P, C_N])
        ident = cst[:, C_ID:C_ID + P]
        x_all = sb("x_all", [P, B, D])
        ctx_all = sb("ctx_all", [P, B, D])
        mask_i = sb("mask_i", [P, T], I32)
        keep = sb("keep", [P, 2, T])
        nokeep = sb("nokeep", [P, 2, T], F32R)
        w_nat = sb("w_nat", [P, 4, D])
        wg_nat = sb("wg_nat", [P, D])
        w_hi = sb("w_hi", [P, 2, D], F32R)
        w_lo = sb("w_lo", [P, 2, D], F32R)
        ws_hi = sb("ws_hi", [P, 2, NG, P], F32R)
        ws_lo = sb("ws_lo", [P, 2, NG, P], F32R)
        wvT = sb("wvT", [P, D])
        wo_s = sb("wo_s", [P, 2, D])
        wg_hi = sb("wg_hi", [P, E], F32R)
        wg_lo = sb("wg_lo", [P, E], F32R)
        bias_w = sb("bias_w", [P, P], F32R)
        ones_b = sb("ones_b", [P, QB, P], F32R)
        stats = sb("stats", [P, QB, 6])
        mv = sb("mv", [P, QB, 2])
        ve = sb("ve", [P, QB])
        rstd = sb("rstd", [P, QB])
        halves = sb("halves", [P, QB])
        xn = sb("xn", [P, QB, D])
        x_hi = sb("x_hi", [P, T], F32R)
        x_lo = sb("x_lo", [P, T], F32R)
        cT = sb("cT", [P, T])
        ck = sb("ck", [P, T])
        ck_hi = sb("ck_hi", [P, T], F32R)
        ck_lo = sb("ck_lo", [P, T], F32R)
        st_hi = sb("st_hi", [P, 2, T], F32R)
        st = sb("st", [P, 2, 2, NG, T], F32R)
        bd = sb("bd", [P, 6, NG * NJ * P], F32R)
        m_neg = sb("m_neg", [P, QB * H])
        m_hi = sb("m_hi", [P, QB * H], F32R)
        m_hl = sb("m_hl", [P, 2, QB * H])
        m_bd = sb("m_bd", [P, H, P], F32R)
        big = sb("big", [P, 4, 2048])
        zs = sb("zs", [P, 2 * P])
        on = sb("on", [P, 2, 2 * P])
        lg = sb("lg", [P, QB, E])
        lsum = sb("lsum", [P, QB])
        sel = sb("sel", [P, QB, E])
        dif = sb("dif", [P, QB, E])
        rank = sb("rank", [P, QB, E])
        th = sb("th", [P, QB, E])
        ew = sb("ew", [P, QB, E])
        ew_hi = sb("ew_hi", [P, QB, E], F32R)
        ew_p = sb("ew_p", [P, QB, P])
        ewT = sb("ewT", [P, T], F32R)
        raw13 = sb("raw13", [P, 2, NB * P])

        prob = [big[:, k, :].rearrange("p (h q) -> p h q", h=H) for k in range(2)]
        va = [big[:, 2 + k, 0:QB * H * R].rearrange("p (m r) -> p m r", r=R) for k in range(2)]

        def bd_slot(k, n):
            return bd[:, 3 * (1 - k) + n % 3, :].rearrange("p (g j q) -> p g j q", g=NG, j=NJ)

        wt = bd[:, :, :].rearrange("p w (k c) -> p w k c", k=NB)
        raw = [raw13[:, 0, :], raw13[:, 1, :], ctx_all[:, :, :].rearrange("p b d -> p (b d)")]
        sel_e = m_bd[:, 0:E, :]
        wo_p = ck[:, 0:2 * P].rearrange("p (s r) -> p s r", s=2)
        y_sb = cT
        o_sb = ck[:, :].rearrange("p (b d) -> p b d", b=QB)
        gt, eq = (keep[:, 0, k * QB * E * E:(k + 1) * QB * E * E].rearrange("p (b e f) -> p b e f", b=QB, e=E) for k in range(2))
        flat = st[:, :, :, :, :].rearrange("p a b g t -> p (a b g) t")
        g_hi = [flat[:, k, :] for k in range(RH)]
        g_lo = [flat[:, RH + k, :] for k in range(RH)]
        x2_hi = [flat[:, 2 * RH + k, :] for k in range(2)]
        x2_lo = [flat[:, 2 * RH + 2 + k, :] for k in range(2)]
        work = big[:, :, :].rearrange("p a (b t) -> p (a b) t", t=T)
        sil = [work[:, k, :] for k in range(3)]
        silw = [work[:, 3 + k, :] for k in range(3)]
        gg = [work[:, 6 + k, :] for k in range(3)]
        ewb = [work[:, 9 + k, :] for k in range(3)]

        bank = [stack.enter_context(nc.psum_tensor(f"bank{k}", [P, 512], F32)) for k in range(8)]

        def work_bank(name):
            return bank[6 + slot[name] % 2]

        s1 = [bank[0], bank[1]]
        s2 = [bank[2], bank[3]]
        ob = [bank[4], bank[5]]
        h1 = [bank[0], bank[1]]
        h3 = [bank[2], bank[3]]
        yb, eb = bank[4], bank[5]

        in_c, in_w, in_wg, in_raw = sem("in_c"), sem("in_w"), sem("in_wg"), sem("in_raw")
        in_x = [sem(f"in_x{k}") for k in range(NQ)]
        in_ctx = [sem(f"in_ctx{k}") for k in range(NQ)]
        in_mask = [sem(f"in_mask{k}") for k in range(NQ)]
        out_done = sem("out_done")
        work_full = sem("work_full")
        work_taken = sem("work_taken")
        dve_done = sem("dve_done")
        pool_done = sem("pool_done")
        cleared = sem("cleared")
        wT_hi_ready = sem("wT_hi_ready")
        wo_p_ready = sem("wo_p_ready")
        ws_ready = sem("ws_ready")
        setup_ready = sem("setup_ready")
        mask_ready = sem("mask_ready")
        var_ready = sem("var_ready")
        rstd_ready = sem("rstd_ready")
        xn_ready = sem("xn_ready")
        xhi_ready = sem("xhi_ready")
        ck_ready = sem("ck_ready")
        ckhi_ready, cklo_ready = sem("ckhi_ready"), sem("cklo_ready")
        sthi_ready = sem("sthi_ready")
        bd_cleared = sem("bd_cleared")
        kbd_ready = [sem(f"kbd_ready{k}") for k in range(3)]
        qbd_ready = [sem(f"qbd_ready{k}") for k in range(3)]
        s1_full, max_done = sem("s1_full"), sem("max_done")
        mhl_ready = sem("mhl_ready")
        s2_full, prob_ready = sem("s2_full"), sem("prob_ready")
        o_full, on_ready = sem("o_full"), sem("on_ready")
        y_full, x2_done = sem("y_full"), sem("x2_done")
        whi_ready = sem("whi_ready")
        x2hi_ready = sem("x2hi_ready")
        dif_ready, th_ready, ewp_ready = sem("dif_ready"), sem("th_ready"), sem("ewp_ready")
        eb_full, ewb_ready = sem("eb_full"), sem("ewb_ready")
        h1_full, h3_full = sem("h1_full"), sem("h3_full")
        sil_ready, silw_ready, gg_ready = sem("sil_ready"), sem("silw_ready"), sem("gg_ready")
        ghi_ready, glo_ready = sem("ghi_ready"), sem("glo_ready")
        down_done = sem("down_done")
        ysb_ready = sem("ysb_ready")

        def taken(engine, name):
            engine.wait_ge(work_taken, slot[name] + 1)

        def diagonal_in(engine, k, n):
            engine.wait_ge((kbd_ready if k else qbd_ready)[n % 3], 16 * NJ * (n // 3 + 1))

        x_d = x.rearrange("(u b) s d -> u s b d", b=QB)
        ctx_d = ctx_in.rearrange("(u b) s d -> u s b d", b=QB)
        out_d = out.rearrange("(u b) s d -> u s b d", b=QB)
        mask_d = mask.rearrange("(u b) s -> u (b s)", b=QB)

        block = stack.enter_context(nc.Block())

        @block.sync
        def _(sp):
            def load(u):
                sp.dma_start(x_all[:, QB * u:QB * (u + 1), :], x_d[u]).then_inc(in_x[u], 16)
                sp.dma_start(ctx_all[:, QB * u:QB * (u + 1), :], ctx_d[u]).then_inc(in_ctx[u], 16)

            load(0)
            sp.dma_start(cst[:, :], consts).then_inc(in_c, 16)
            for k, w in enumerate((Wq, Wk, Wv, Wo)):
                sp.dma_start(w_nat[:, k, :], w).then_inc(in_w, 16)
            sp.dma_start(wg_nat[0:E, :], wg).then_inc(in_wg, 16)
            for u in range(1, NQ):
                load(u)
            for k, w in enumerate((w1, w3)):
                sp.dma_start(raw[k].rearrange("p (k h) -> p k h", k=NB),
                             w.rearrange("e (c p) h -> p (e c) h", p=P)).then_inc(in_raw, 16)

            def block_diagonal(k, n):
                u, b = divmod(n, QB)
                taken(sp, ("st", u, (K_STACKS if k else Q_STACKS) - 1))
                if n >= 3:
                    sp.wait_ge(s1_full if k else s2_full, NG * (n - 2))
                else:
                    sp.wait_ge(bd_cleared, 3 if k else 6)
                for j in range(NJ):
                    rows = slice(R * j, R * (j + 1))
                    sp.dma_start(bd_slot(k, n)[rows, :, j, :].bitcast(F32), st[rows, u % 2, k, :, b * S:(b + 1) * S].bitcast(F32)
                                 ).then_inc((kbd_ready if k else qbd_ready)[n % 3], 16)

            for u in range(NQ + 1):
                if u == NQ:
                    sp.wait_ge(work_full, slot["cT", NQ - 1] + 1)
                    sp.dma_start(raw[2].rearrange("p (e i) -> p e i", e=E), w2.rearrange("e h i -> h e i")).then_inc(in_raw, 16)
                for b in range(QB):
                    if u < NQ:
                        block_diagonal(1, QB * u + b)
                    if u >= 1 and b < 2:
                        block_diagonal(0, QB * (u - 1) + 2 + b)
                if u < NQ:
                    block_diagonal(0, QB * u)
                    block_diagonal(0, QB * u + 1)
            for q in range(NQ):
                taken(sp, ("yT", q))
                sp.dma_start(out_d[q], o_sb).then_inc(out_done, 16)
            sp.wait_ge(out_done, 16 * NQ)

        @block.tensor
        def _(pe):
            def claim(name):
                n = slot[name]
                if n >= 2:
                    pe.wait_ge(work_taken, n - 1)
                return work_bank(name)

            def split_product(o, w_parts, m_parts, extra=None):
                pairs = [(w_parts[0], m_parts[0]), (w_parts[0], m_parts[1]), (w_parts[1], m_parts[0])]
                if extra is not None:
                    pairs.append(extra)
                for k, (w, m) in enumerate(pairs):
                    last = nc.tensor.matmul(o, w, m, start=(k == 0), stop=(k == len(pairs) - 1))
                return last

            def transpose4(name, pieces):
                o = claim(name)
                for k, piece in enumerate(pieces):
                    last = nc.tensor.transpose(o[0:piece.shape[1], P * k:P * k + piece.shape[0]], piece,
                                               ident[0:piece.shape[0], 0:piece.shape[0]])
                last.then_inc(work_full, 1)

            pe.wait_ge(in_c, 16)
            pe.wait_ge(in_w, 64)
            pe.wait_ge(in_wg, 16)
            transpose4("w", [w_nat[:, 0, :], w_nat[:, 1, :], w_nat[:, 2, :], wg_nat[0:E, :]])
            pe.wait_ge(wo_p_ready, 1)
            transpose4("wo", [wo_p[:, 0, :], wo_p[:, 1, :]])

            def project_out(n):
                pe.wait_ge(on_ready, n + 1)
                o = ob[n % 2][:, 256:384]
                for s in range(2):
                    last = nc.tensor.matmul(o, on[:, n % 2, s * P:(s + 1) * P], wo_s[:, s, :], start=(s == 0), stop=(s == 1))
                last.then_inc(y_full, 1)

            def front(u):
                if u < NQ:
                    pe.wait_ge(in_ctx[u], 16)
                    transpose4(("cT", u), [ctx_all[:, QB * u + b, :] for b in range(QB)])
                    pe.wait_ge(xn_ready, u + 1)
                    transpose4(("xT", u), [xn[:, b, :] for b in range(QB)])
                if u >= 2:
                    project_out(QB * (u - 1) - 1)
                if u >= 1:
                    pe.wait_ge(mhl_ready, u)
                    transpose4(("MT", u - 1), [m_hl[:, :, :].rearrange("p a m -> p (a m)")])
                if u == NQ:
                    return
                o = claim(("V", u))
                taken(pe, ("cT", u))
                if u == 0:
                    pe.wait_ge(setup_ready, 1)
                for b in range(QB):
                    last = nc.tensor.matmul(o[:, b * D:(b + 1) * D], cT[:, b * S:(b + 1) * S], wvT[:, :], start=True, stop=True)
                last.then_inc(work_full, 1)
                for k, (is_k, g) in enumerate(STACKS):
                    o = claim(("st", u, k))
                    if k == 0:
                        taken(pe, ("xT", u))
                        if u == 0:
                            pe.wait_ge(ws_ready, 1)
                    if is_k and g == 0:
                        pe.wait_ge(cklo_ready, u + 1)
                        pe.wait_ge(mask_ready, u + 1)
                    parts = (ws_hi[:, is_k, g, :], ws_lo[:, is_k, g, :])
                    if is_k:
                        last = split_product(o[:, :], parts, (ck_hi[:, :], ck_lo[:, :]), (bias_w[:, :], nokeep[:, u % 2, :]))
                    else:
                        last = split_product(o[:, :], parts, (x_hi[:, :], x_lo[:, :]))
                    last.then_inc(work_full, 1)

            def values(n, g):
                if g == 0 and n >= 2:
                    pe.wait_ge(x2_done, n - 1)
                if g == 0 and n % QB == 0:
                    taken(pe, ("V", n // QB))
                pe.wait_ge(prob_ready, NG * n + g + 1)
                half, i = g // 2, g % 2
                for j in range(NJ):
                    last = nc.tensor.matmul(ob[n % 2][R * j:R * (j + 1), half * P:(half + 1) * P],
                                            va[(n // QB) % 2][:, ((n % QB) * 4 + half * 2 + i) * NJ + j, :],
                                            prob[n % 2][:, NJ * g + j, :], start=(i == 0), stop=(i == 1),
                                            tile_position=(0, R * j))
                if g == NG - 1:
                    last.then_inc(o_full, 1)

            for u in range(NQ + 1):
                front(u)
                for b in range(QB):
                    for g in range(NG):
                        if u >= 1:
                            n = QB * (u - 1) + b
                            k = NG * n + g
                            if g == 0:
                                diagonal_in(pe, 0, n)
                                if b == 0:
                                    taken(pe, ("MT", u - 1))
                            if k >= 2:
                                pe.wait_ge(prob_ready, k - 1)
                            nc.tensor.matmul(s2[k % 2][:, :], ones_b[:, b, :],
                                             m_bd[:, NJ * g:NJ * (g + 1), :].rearrange("p h q -> p (h q)"),
                                             start=True, stop=False)
                            nc.tensor.matmul(s2[k % 2][:, :], st[:, (u - 1) % 2, 1, g, b * S:(b + 1) * S],
                                             bd_slot(0, n)[:, g, :, :].rearrange("p j q -> p (j q)"),
                                             start=False, stop=True).then_inc(s2_full, 1)
                        if u < NQ:
                            n = QB * u + b
                            k = NG * n + g
                            if g == 0:
                                if b == 0:
                                    taken(pe, ("st", u, Q_STACKS - 1))
                                diagonal_in(pe, 1, n)
                            if k >= 2:
                                pe.wait_ge(max_done, k - 1)
                            nc.tensor.matmul(s1[k % 2][:, :], st[:, u % 2, 0, g, b * S:(b + 1) * S],
                                             bd_slot(1, n)[:, g, :, :].rearrange("p j q -> p (j q)"),
                                             start=True, stop=True).then_inc(s1_full, 1)
                        if u >= 1 and b >= 1:
                            values(QB * (u - 1) + b - 1, g)
                            if g == 1 and b >= 2:
                                project_out(QB * (u - 1) + b - 2)
                if u >= 1:
                    for g in range(NG):
                        values(QB * u - 1, g)
                    project_out(QB * u - 2)
            project_out(B - 1)

            pe.wait_ge(in_raw, 48)
            pe.wait_ge(x2_done, B)
            for k in range(3 * NB // 4):
                transpose4(("W", k), [raw[k // 4][:, (4 * (k % 4) + m) * P:(4 * (k % 4) + m + 1) * P] for m in range(4)])

            def prepare_xT(q):
                pe.wait_ge(xn_ready, NQ + q + 1)
                transpose4(("x2T", q), [xn[:, b, :] for b in range(QB)])

            def prepare_logits(q):
                o = claim(("lg", q))
                taken(pe, ("x2T", q))
                for b in range(QB):
                    t = slice(b * S, (b + 1) * S)
                    last = split_product(o[:, b * E:(b + 1) * E], (x2_hi[q % 2][:, t], x2_lo[q % 2][:, t]), (wg_hi[:, :], wg_lo[:, :]))
                last.then_inc(work_full, 1)

            def prepare_weights(q):
                pe.wait_ge(ewp_ready, q + 1)
                transpose4(("ewT", q), [ew_p[:, b, :] for b in range(QB)])

            def down(n):
                q, k = divmod(n, NB)
                if k == 0 and q:
                    pe.wait_ge(ysb_ready, q)
                pe.wait_ge(glo_ready, n + 1)
                for c, (a, g) in enumerate(((4, g_hi), (4, g_lo), (5, g_hi))):
                    last = nc.tensor.matmul(yb[:, :], wt[:, a, k, :], g[n % RH], start=(k == 0 and c == 0), stop=(k == NB - 1 and c == 2))
                last.then_inc(down_done, 1)

            pe.wait_ge(setup_ready, 2)
            prepare_xT(0)
            prepare_logits(0)
            prepare_weights(0)
            taken(pe, ("W", 3 * NB // 4 - 1))
            for n in range(NQ * NB):
                q, k = divmod(n, NB)
                e = k // 2
                if k == 0:
                    taken(pe, ("ewT", q))
                if k % 2 == 0:
                    if n:
                        pe.wait_ge(ewb_ready, n // 2)
                    nc.tensor.matmul(eb[:, :], sel_e[:, e, :], ewT[:, :], start=True, stop=True).then_inc(eb_full, 1)
                if n >= 2:
                    pe.wait_ge(sil_ready, n - 1)
                split_product(h1[n % 2][:, :], (wt[:, 0, k, :], wt[:, 1, k, :]), (x2_hi[q % 2], x2_lo[q % 2])).then_inc(h1_full, 1)
                if n >= 2:
                    pe.wait_ge(gg_ready, n - 1)
                split_product(h3[n % 2][:, :], (wt[:, 2, k, :], wt[:, 3, k, :]), (x2_hi[q % 2], x2_lo[q % 2])).then_inc(h3_full, 1)
                if n >= LAG:
                    down(n - LAG)
                if k == 5 and q:
                    pe.wait_ge(ysb_ready, q)
                    transpose4(("yT", q - 1), [y_sb[:, b * S:(b + 1) * S] for b in range(QB)])
                if q + 1 < NQ:
                    if k == 8:
                        prepare_xT(q + 1)
                    if k == 10:
                        prepare_logits(q + 1)
                    if k == 14:
                        prepare_weights(q + 1)
            for n in range(NQ * NB - LAG, NQ * NB):
                down(n)
            pe.wait_ge(ysb_ready, NQ)
            transpose4(("yT", NQ - 1), [y_sb[:, b * S:(b + 1) * S] for b in range(QB)])

        @block.scalar
        def _(act):
            def copy(o, i):
                return nc.scalar.activation(o, i, ACT.Copy)

            def full(name):
                act.wait_ge(work_full, slot[name] + 1)

            full("w")
            wb = work_bank("w")
            copy(w_hi[:, :, :].rearrange("p a d -> p (a d)"), wb[:, 0:2 * D]).then_inc(wT_hi_ready, 1)
            copy(wg_hi[:, :], wb[:, 3 * P:3 * P + E]).then_inc(wT_hi_ready, 1)

            for u in range(NQ + 1):
                if u < NQ:
                    full(("xT", u))
                    if u:
                        act.wait_ge(work_full, slot["st", u - 1, 2 * NG - 1] + 1)
                    copy(x_hi[:, :], work_bank(("xT", u))[:, :]).then_inc(xhi_ready, 1)
                    act.wait_ge(ck_ready, u + 1)
                    copy(ck_hi[:, :], ck[:, :]).then_inc(ckhi_ready, 1)
                    for k, (is_k, g) in enumerate(STACKS):
                        n = Q_STACKS * u + k
                        full(("st", u, k))
                        if k >= 2:
                            taken(act, ("st", u, k - 2))
                        elif u:
                            taken(act, ("st", u - 1, Q_STACKS + k - 2))
                        src = work_bank(("st", u, k))[:, :]
                        if is_k:
                            i = copy(st_hi[:, n % 2, :], src)
                        else:
                            i = nc.scalar.activation(st_hi[:, n % 2, :], src, ACT.Identity, bias=cst[:, C_ONE:C_ONE + 1])
                        i.then_inc(sthi_ready, 1)
                if u >= 1:
                    for b in range(QB):
                        for g in range(NG):
                            n = QB * (u - 1) + b
                            k = NG * n + g
                            act.wait_ge(s2_full, k + 1)
                            if g == 0 and n >= 2:
                                act.wait_ge(o_full, n - 1)
                            nc.scalar.activation(prob[n % 2][:, NJ * g:NJ * (g + 1), :].rearrange("p h q -> p (h q)"),
                                                 s2[k % 2][:, :], ACT.Exp, scale=SCALE).then_inc(prob_ready, 1)

            act.wait_ge(y_full, B)
            for k in range(3 * NB // 4):
                full(("W", k))
                copy(wt[:, 2 * (k // 4), 4 * (k % 4):4 * (k % 4) + 4, :].rearrange("p k c -> p (k c)"),
                     work_bank(("W", k))[:, :]).then_inc(whi_ready, 1)

            def prepare(q):
                full(("x2T", q))
                if q >= 2:
                    act.wait_ge(h3_full, NB * (q - 1))
                copy(x2_hi[q % 2], work_bank(("x2T", q))[:, :]).then_inc(x2hi_ready, 1)

            def round_hidden(n):
                act.wait_ge(gg_ready, n + 1)
                if n >= RH:
                    act.wait_ge(down_done, n - RH + 1)
                copy(g_hi[n % RH], gg[n % 3]).then_inc(ghi_ready, 1)

            def take_y(q):
                act.wait_ge(down_done, NB * (q + 1))
                if q:
                    act.wait_ge(work_full, slot["yT", q - 1] + 1)
                copy(y_sb[:, :], yb[:, :]).then_inc(ysb_ready, 1)

            def squash(q):
                act.wait_ge(dif_ready, q + 1)
                nc.scalar.activation(th[:, :, :], dif[:, :, :], ACT.Tanh, scale=0.5).then_inc(th_ready, 1)

            prepare(0)
            squash(0)
            for n in range(NQ * NB):
                q, k = divmod(n, NB)
                if k % 2 == 0:
                    m = n // 2
                    act.wait_ge(eb_full, m + 1)
                    if m >= 3:
                        act.wait_ge(silw_ready, 2 * (m - 2))
                    copy(ewb[m % 3], eb[:, :]).then_inc(ewb_ready, 1)
                act.wait_ge(h1_full, n + 1)
                if n >= 3:
                    act.wait_ge(silw_ready, n - 2)
                nc.scalar.activation(sil[n % 3], h1[n % 2][:, :], ACT.Silu).then_inc(sil_ready, 1)
                if n:
                    round_hidden(n - 1)
                if k == LAG - 1 and q:
                    take_y(q - 1)
                if k == 9 and q + 1 < NQ:
                    prepare(q + 1)
                if k == 12 and q + 1 < NQ:
                    squash(q + 1)
            round_hidden(NQ * NB - 1)
            take_y(NQ - 1)

        @block.gpsimd
        def _(pool):
            steps = [0]

            def own(ins):
                steps[0] += 1
                ins.then_inc(pool_done, 1)
                pool.wait_ge(pool_done, steps[0])

            def load_mask(u):
                if u:
                    pool.wait_ge(mask_ready, u)
                pool.dma_start(mask_i[:, :], mask_d[u].partition_broadcast(P)).then_inc(in_mask[u], 16)

            load_mask(0)
            nc.gpsimd.memset(halves[:, :], -0.5)
            nc.gpsimd.memset(wo_p[:, :, :], 0.0).then_inc(cleared, 1)
            nc.gpsimd.memset(ws_hi[:, :, :, :].bitcast(F32), 0.0)
            nc.gpsimd.memset(ws_lo[:, :, :, :].bitcast(F32), 0.0)
            for k in (0, 1, 2):
                nc.gpsimd.memset(bd[:, k, :].bitcast(F32), 0.0).then_inc(bd_cleared, 1)

            def inverse_deviation(m):
                pool.wait_ge(var_ready, m + 1)
                own(nc.gpsimd.tensor_scalar(ve[:, :], mv[:, :, 1], EPS, None, ALU.add))
                nc.gpsimd.tensor_tensor(rstd[:, :], ve[:, :], halves[:, :], ALU.pow).then_inc(rstd_ready, 1)

            inverse_deviation(0)
            pool.wait_ge(wT_hi_ready, 1)
            taken(pool, "w")
            for k in range(2):
                for src, dst in ((w_hi, ws_hi), (w_lo, ws_lo)):
                    for t in range(3):
                        last = nc.gpsimd.tensor_copy(
                            dst[:, k, :, :].rearrange("p g (j r) -> p (g j) r", j=NJ)[:, :, HD * t:HD * (t + 1)],
                            src[:, k, :].rearrange("p (h d) -> p h d", d=HD))
            last.then_inc(ws_ready, 1)
            for k in (3, 4, 5):
                nc.gpsimd.memset(bd[:, k, :].bitcast(F32), 0.0).then_inc(bd_cleared, 1)

            for u in range(NQ):
                taken(pool, ("cT", u))
                pool.wait_ge(mask_ready, u + 1)
                if u:
                    pool.wait_ge(cklo_ready, u)
                nc.gpsimd.tensor_tensor(ck[:, :], cT[:, :], keep[:, u % 2, :], ALU.mult).then_inc(ck_ready, 1)
                if u + 1 < NQ:
                    load_mask(u + 1)
                    inverse_deviation(u + 1)

            inverse_deviation(NQ)
            for n in range(NQ * NB):
                q, k = divmod(n, NB)
                pool.wait_ge(sil_ready, n + 1)
                pool.wait_ge(ewb_ready, n // 2 + 1)
                if n >= 3:
                    pool.wait_ge(gg_ready, n - 2)
                nc.gpsimd.tensor_tensor(silw[n % 3], sil[n % 3], ewb[(n // 2) % 3], ALU.mult).then_inc(silw_ready, 1)
                if k == 5 and q + 1 < NQ:
                    inverse_deviation(NQ + q + 1)

        @block.vector
        def _(dve):
            steps = [0]

            def mark(ins):
                steps[0] += 1
                ins.then_inc(dve_done, 1)
                return steps[0]

            def own(ins):
                dve.wait_ge(dve_done, mark(ins))

            def full(name):
                dve.wait_ge(work_full, slot[name] + 1)

            def statistics(n0, m):
                if m:
                    dve.wait_ge(xn_ready, m)
                for b in range(QB):
                    last = mark(nc.vector.bn_stats(stats[:, b, :], x_all[:, n0 + b, :]))
                dve.wait_ge(dve_done, last)
                for b in range(QB):
                    ins = nc.vector.bn_aggr(mv[:, b, :], stats[:, b, :])
                    last = mark(ins) if b < QB - 1 else last
                ins.then_inc(var_ready, 1)

            def normalise(n0, m):
                dve.wait_ge(rstd_ready, m + 1)
                for b in range(QB):
                    last = nc.vector.tensor_scalar(xn[:, b, :], x_all[:, n0 + b, :], mv[:, b, 0:1], rstd[:, b:b + 1],
                                                   ALU.subtract, ALU.mult)
                last.then_inc(xn_ready, 1)

            def masks(u):
                dve.wait_ge(in_mask[u], 16)
                if u >= 2:
                    dve.wait_ge(work_full, slot["st", u - 2, Q_STACKS - 1] + 1)
                    dve.wait_ge(ck_ready, u - 1)
                own(nc.vector.tensor_scalar(nokeep[:, u % 2, :], mask_i[:, :], 0, None, ALU.is_equal))
                nc.vector.tensor_scalar(keep[:, u % 2, :], nokeep[:, u % 2, :].bitcast(F32), -1.0, 1.0, ALU.mult, ALU.add
                                        ).then_inc(mask_ready, 1)

            nc.vector.memset(ew_p[:, :, :], 0.0)
            for k in range(2):
                own(nc.vector.memset(va[k][:, :, :], 0.0))
            for k in range(2):
                v = va[k].rearrange("p (m i j) r -> p m i j r", i=2, j=NJ)
                own(nc.vector.memset(v[:, :, 0, :, 16:17], 1.0))
                own(nc.vector.memset(v[:, :, 1, :, 17:18], 1.0))
            dve.wait_ge(in_x[0], 16)
            statistics(0, 0)
            dve.wait_ge(in_c, 16)
            dve.wait_ge(in_w, 64)
            dve.wait_ge(cleared, 1)
            for s in range(2):
                for i in range(2):
                    c0 = (2 * s + i) * NJ * HD
                    last = nc.vector.tensor_copy(wo_p[:, s, :].rearrange("p (j r) -> p j r", r=R)[:, :, HD * i:HD * (i + 1)],
                                                 w_nat[:, 3, c0:c0 + NJ * HD].rearrange("p (j d) -> p j d", d=HD))
            last.then_inc(wo_p_ready, 1)
            normalise(0, 0)
            full("w")
            wb = work_bank("w")
            dve.wait_ge(wT_hi_ready, 2)
            nc.vector.tensor_copy(wvT[:, :], wb[:, 2 * P:3 * P])
            nc.vector.tensor_tensor(wg_lo[:, :], wb[:, 3 * P:3 * P + E], wg_hi[:, :].bitcast(F32), ALU.subtract)
            nc.vector.tensor_tensor(w_lo[:, :, :].rearrange("p a d -> p (a d)"), wb[:, 0:2 * D],
                                    w_hi[:, :, :].rearrange("p a d -> p (a d)").bitcast(F32), ALU.subtract).then_inc(work_taken, 1)
            full("wo")
            nc.vector.tensor_copy(wo_s[:, :, :].rearrange("p a d -> p (a d)"), work_bank("wo")[:, 0:2 * D]).then_inc(work_taken, 1)
            nc.vector.tensor_copy(bias_w[:, :], cst[:, C_BIAS:C_BIAS + P])
            nc.vector.tensor_copy(ones_b[:, :, :], cst[:, C_BATCH:C_BATCH + QB].unsqueeze(2).to_broadcast([P, QB, P])
                                  ).then_inc(setup_ready, 1)
            masks(0)

            def take_projection(n):
                dve.wait_ge(y_full, n + 1)
                nc.vector.tensor_tensor(x_all[:, n, :], ob[n % 2][:, 256:384], x_all[:, n, :], ALU.add).then_inc(x2_done, 1)

            def normalise_heads(n):
                dve.wait_ge(o_full, n + 1)
                own(nc.vector.stream_shuffle(zs[:, :], ob[n % 2][:, 0:2 * P], [16] * 8 + [17] * 8 + [16] * 16))
                own(nc.vector.reciprocal(zs[:, :], zs[:, :]))
                if n >= 2:
                    dve.wait_ge(y_full, n - 1)
                nc.vector.tensor_tensor(on[:, n % 2, :], ob[n % 2][:, 0:2 * P], zs[:, :], ALU.mult).then_inc(on_ready, 1)

            def round_maxima():
                own(nc.vector.tensor_copy(m_hi[:, :], m_neg[:, :]))
                nc.vector.tensor_copy(m_hl[:, 0, :], m_hi[:, :].bitcast(F32))
                nc.vector.tensor_tensor(m_hl[:, 1, :], m_neg[:, :], m_hi[:, :].bitcast(F32), ALU.subtract).then_inc(mhl_ready, 1)

            for u in range(NQ + 1):
                if u < NQ:
                    full(("cT", u))
                    if u:
                        dve.wait_ge(ck_ready, u)
                        dve.wait_ge(work_full, slot["V", u - 1] + 1)
                    nc.vector.tensor_copy(cT[:, :], work_bank(("cT", u))[:, :]).then_inc(work_taken, 1)
                    full(("xT", u))
                    dve.wait_ge(xhi_ready, u + 1)
                    if u:
                        dve.wait_ge(work_full, slot["st", u - 1, 2 * NG - 1] + 1)
                    nc.vector.tensor_tensor(x_lo[:, :], work_bank(("xT", u))[:, :], x_hi[:, :].bitcast(F32),
                                            ALU.subtract).then_inc(work_taken, 1)
                if u >= 2:
                    take_projection(QB * (u - 1) - 1)
                if u >= 1:
                    full(("MT", u - 1))
                    if u >= 2:
                        dve.wait_ge(s2_full, NG * QB * (u - 1))
                    mt = work_bank(("MT", u - 1))[:, 0:P]
                    nc.vector.tensor_tensor(m_bd[:, :, :], mt.unsqueeze(1).to_broadcast([P, H, P]),
                                            cst[:, C_HEAD:C_HEAD + H].unsqueeze(2).to_broadcast([P, H, P]),
                                            ALU.mult).then_inc(work_taken, 1)
                if u < NQ:
                    full(("V", u))
                    if u >= 2:
                        dve.wait_ge(o_full, QB * (u - 1))
                    src = work_bank(("V", u))[:, :].rearrange("p (m i j d) -> p m i j d", i=2, j=NJ, d=HD)
                    dst = va[u % 2].rearrange("p (m i j) r -> p m i j r", i=2, j=NJ)
                    for i in range(2):
                        last = nc.vector.tensor_copy(dst[:, :, i, :, HD * i:HD * (i + 1)], src[:, :, i, :, :])
                    last.then_inc(work_taken, 1)
                    dve.wait_ge(ckhi_ready, u + 1)
                    nc.vector.tensor_tensor(ck_lo[:, :], ck[:, :], ck_hi[:, :].bitcast(F32), ALU.subtract).then_inc(cklo_ready, 1)
                    if u >= 2:
                        dve.wait_ge(s1_full, NG * QB * (u - 1))
                        dve.wait_ge(s2_full, NG * QB * (u - 1))
                        for n in range(QB * (u - 1) - 3, QB * (u - 1)):
                            diagonal_in(dve, 1, n)
                            diagonal_in(dve, 0, n)
                    for k, (is_k, g) in enumerate(STACKS):
                        n = Q_STACKS * u + k
                        full(("st", u, k))
                        dve.wait_ge(sthi_ready, n + 1)
                        nc.vector.scalar_tensor_tensor(
                            st[:, u % 2, is_k, g, :], st_hi[:, n % 2, :].bitcast(F32),
                            cst[:, (C_CK if is_k else C_CQ):(C_CK if is_k else C_CQ) + 1],
                            work_bank(("st", u, k))[:, :], ALU.mult, ALU.add).then_inc(work_taken, 1)
                for b in range(QB):
                    if u < NQ:
                        for g in range(NG):
                            k = NG * (QB * u + b) + g
                            dve.wait_ge(s1_full, k + 1)
                            nc.vector.tensor_reduce(m_neg[:, H * b + NJ * g:H * b + NJ * (g + 1)],
                                                    s1[k % 2][:, :].rearrange("p (j q) -> p j q", j=NJ), X, ALU.max,
                                                    negate=True).then_inc(max_done, 1)
                    if u >= 1 and b >= 1:
                        normalise_heads(QB * (u - 1) + b - 1)
                    if u >= 1 and b >= 2:
                        take_projection(QB * (u - 1) + b - 2)
                    if u + 1 < NQ:
                        if b == 1:
                            dve.wait_ge(in_x[u + 1], 16)
                            statistics(QB * (u + 1), u + 1)
                        if b == 2:
                            normalise(QB * (u + 1), u + 1)
                            masks(u + 1)
                if u < NQ:
                    dve.wait_ge(max_done, NG * QB * (u + 1))
                    round_maxima()
                if u >= 1:
                    normalise_heads(QB * u - 1)
                    take_projection(QB * u - 2)
            take_projection(B - 1)

            def second_statistics(q):
                dve.wait_ge(x2_done, QB * (q + 1))
                statistics(QB * q, NQ + q)

            def split_x2(q):
                full(("x2T", q))
                dve.wait_ge(x2hi_ready, q + 1)
                if q >= 2:
                    dve.wait_ge(h3_full, NB * (q - 1))
                nc.vector.tensor_tensor(x2_lo[q % 2], work_bank(("x2T", q))[:, :], x2_hi[q % 2].bitcast(F32),
                                        ALU.subtract).then_inc(work_taken, 1)

            def route(q):
                full(("lg", q))
                nc.vector.tensor_copy(lg[:, :, :].rearrange("p b e -> p (b e)"),
                                      work_bank(("lg", q))[:, 0:QB * E]).then_inc(work_taken, 1)
                taken(dve, ("lg", q))
                other = lg[:, :, :].unsqueeze(2).to_broadcast([P, QB, E, E])
                this = lg[:, :, :].unsqueeze(3).to_broadcast([P, QB, E, E])
                lower = cst[:, C_LOW:C_LOW + E * E].rearrange("p (e f) -> p e f", e=E)
                for b in range(QB):
                    last = mark(nc.vector.tensor_tensor(gt[:, b], other[:, b], this[:, b], ALU.is_gt))
                    last = mark(nc.vector.tensor_tensor(eq[:, b], other[:, b], this[:, b], ALU.is_equal))
                dve.wait_ge(dve_done, last)
                for b in range(QB):
                    last = mark(nc.vector.tensor_tensor(eq[:, b], eq[:, b], lower, ALU.mult))
                dve.wait_ge(dve_done, last)
                own(nc.vector.tensor_tensor(gt, gt, eq, ALU.add))
                own(nc.vector.tensor_reduce(rank[:, :, :], gt, X, ALU.add))

            def compare(q):
                own(nc.vector.tensor_scalar(sel[:, :, :], rank[:, :, :], 2.0, None, ALU.is_lt))
                own(nc.vector.tensor_tensor(ew[:, :, :], sel[:, :, :], lg[:, :, :], ALU.mult))
                own(nc.vector.tensor_reduce(lsum[:, :], ew[:, :, :], X, ALU.add))
                nc.vector.scalar_tensor_tensor(dif[:, :, :], lg[:, :, :], 2.0, lsum[:, :].unsqueeze(2).to_broadcast([P, QB, E]),
                                               ALU.mult, ALU.subtract).then_inc(dif_ready, 1)

            def weigh(q):
                dve.wait_ge(th_ready, q + 1)
                own(nc.vector.tensor_scalar(ew[:, :, :], th[:, :, :], 0.5, 0.5, ALU.mult, ALU.add))
                own(nc.vector.tensor_tensor(ew[:, :, :], ew[:, :, :], sel[:, :, :], ALU.mult))
                own(nc.vector.tensor_copy(ew_hi[:, :, :], ew[:, :, :]))
                nc.vector.tensor_copy(ew_p[:, :, 0:E], ew_hi[:, :, :].bitcast(F32))
                nc.vector.tensor_tensor(ew_p[:, :, E:2 * E], ew[:, :, :], ew_hi[:, :, :].bitcast(F32),
                                        ALU.subtract).then_inc(ewp_ready, 1)

            def take_weights(q):
                full(("ewT", q))
                if q:
                    dve.wait_ge(eb_full, E * q)
                nc.vector.tensor_copy(ewT[:, :], work_bank(("ewT", q))[:, :]).then_inc(work_taken, 1)

            def finish(q):
                full(("yT", q))
                if q:
                    dve.wait_ge(out_done, 16 * q)
                nc.vector.tensor_tensor(o_sb.rearrange("p b d -> p (b d)"), work_bank(("yT", q))[:, :],
                                        x_all[:, QB * q:QB * (q + 1), :].rearrange("p b d -> p (b d)"),
                                        ALU.add).then_inc(work_taken, 1)

            def hidden_rest(n):
                dve.wait_ge(ghi_ready, n + 1)
                dve.wait_ge(gg_ready, n + 1)
                if n >= RH:
                    dve.wait_ge(down_done, n - RH + 1)
                nc.vector.tensor_tensor(g_lo[n % RH], gg[n % 3], g_hi[n % RH].bitcast(F32), ALU.subtract).then_inc(glo_ready, 1)

            nc.vector.tensor_copy(sel_e, cst[:, C_EXP:C_EXP + E].unsqueeze(2).to_broadcast([P, E, P])).then_inc(setup_ready, 1)
            second_statistics(0)
            normalise(0, NQ)
            for k in range(3 * NB // 4):
                full(("W", k))
                dve.wait_ge(whi_ready, k + 1)
                piece = slice(4 * (k % 4), 4 * (k % 4) + 4)
                nc.vector.tensor_tensor(wt[:, 2 * (k // 4) + 1, piece, :].rearrange("p k c -> p (k c)"), work_bank(("W", k))[:, :],
                                        wt[:, 2 * (k // 4), piece, :].rearrange("p k c -> p (k c)").bitcast(F32),
                                        ALU.subtract).then_inc(work_taken, 1)
            split_x2(0)
            route(0)
            compare(0)
            weigh(0)
            take_weights(0)
            for n in range(NQ * NB):
                q, k = divmod(n, NB)
                dve.wait_ge(silw_ready, n + 1)
                dve.wait_ge(h3_full, n + 1)
                if n >= 3:
                    dve.wait_ge(glo_ready, n - 2)
                nc.vector.tensor_tensor(gg[n % 3], silw[n % 3], h3[n % 2][:, :], ALU.mult).then_inc(gg_ready, 1)
                if n:
                    hidden_rest(n - 1)
                if k == 6 and q:
                    finish(q - 1)
                if q + 1 < NQ:
                    if k == 3:
                        second_statistics(q + 1)
                    if k == 7:
                        normalise(QB * (q + 1), NQ + q + 1)
                    if k == 9:
                        split_x2(q + 1)
                    if k == 11:
                        route(q + 1)
                        compare(q + 1)
                    if k == 13:
                        weigh(q + 1)
                    if k == 15:
                        take_weights(q + 1)
            hidden_rest(NQ * NB - 1)
            finish(NQ - 1)


_INS = ["x", "ctx_1024", "mask_BxS2_if1", "L0_xattn_Wq", "L0_xattn_Wk", "L0_xattn_Wv", "L0_xattn_Wo", "L0_ffn_wg",
        "L0_ffn_w1", "L0_ffn_w3", "L0_ffn_w2"]


def kernel(**inputs):
    import concourse.bacc as bacc
    from concourse.bass_utils import run_bass_kernel_spmd

    nc = bacc.Bacc("TRN2", target_bir_lowering=False, num_devices=1)
    arrays = {f"in_{name}": np.ascontiguousarray(inputs[name]) for name in _INS}
    arrays["in_patterns"] = constants()
    args = [nc.dram_tensor(name, a.shape, mybir.dt.from_np(a.dtype), kind="ExternalInput").ap() for name, a in arrays.items()]
    out = nc.dram_tensor("out", (B, S, D), F32, kind="ExternalOutput").ap()
    program(nc, *args, out)
    return run_bass_kernel_spmd(nc, [arrays], core_ids=[0]).results[0]["out"]
```

```python
from contextlib import ExitStack

import numpy as np

import concourse.bass as bass
from concourse import mybir

F32 = mybir.dt.float32
F32R = mybir.dt.float32r
I32 = mybir.dt.int32
ALU = mybir.AluOpType
ACT = mybir.ActivationFunctionType
X = mybir.AxisListType.X

P = 128
B, S, D = 16, 128, 128
H, HD = 16, 8
NG, NJ = 4, 4
R = 32
QB = 4
NQ = B // QB
T = QB * S
E, I = 8, 256
NB = E * I // P
SCALE = float(HD) ** -0.5
NEG = -1.0e9 / SCALE
EPS = 1e-5
LAG = 4
RH = 6
SH = 3


def split_constant(v):
    bits = np.float32(v).view(np.uint32)
    hi = np.uint32(bits & np.uint32(0xFFFFF000)).view(np.float32)
    return float(hi), float(np.float32(np.float32(v) - hi))


C_ID, C_CQ, C_CK, C_ONE, C_HEAD, C_BATCH, C_EXP, C_LOW, C_BIAS, C_N = 0, 128, 129, 130, 132, 148, 152, 160, 224, 352


def constants():
    c = np.zeros((P, C_N), np.float32)
    p = np.arange(P)
    r = p % R
    c[:, C_ID:C_ID + P] = np.eye(P)
    c[:, C_CQ] = np.where((r >= 16) & (r < 24), -1.0, np.where((r == 24) | (r == 25), 1.0, 0.0))
    c[:, C_CK] = np.where((r >= 8) & (r < 16), -1.0, 0.0)
    c[:, C_ONE] = (r == 24) | (r == 25)
    for h in range(H):
        c[:, C_HEAD + h] = p % H == h
    for b in range(QB):
        c[:, C_BATCH + b] = (p // H) % QB == b
    for e in range(E):
        c[:, C_EXP + e] = (p < 2 * E) & (p % E == e)
        c[:, C_LOW + E * e:C_LOW + E * e + e] = 1.0
    hi, lo = split_constant(NEG)
    for j in range(NJ):
        c[0, C_BIAS + R * j + 24] = hi
        c[0, C_BIAS + R * j + 25] = lo
    return c


WORK_BANKS, STACK_BANKS = (6, 7), (0, 1, 6, 7)


def last_fills(tick):
    fills = []
    if tick % 2 == 0 and tick // 2 < NB // 2:
        fills.append(("W", tick // 2))
    if tick >= NG * QB:
        fills.append(("W", NB // 2 + tick - NG * QB))
    if tick == 1:
        fills.append(("lg", 0))
    if tick == 5:
        fills.append(("x2T", 1))
    if tick == 13:
        fills.append(("ewT", 0))
    return fills


def unit_fills(n):
    q, k = divmod(n, NB)
    fills = []
    if 2 <= q + 1 < NQ and k == 1:
        fills.append(("x2T", q + 1))
    if q + 1 < NQ and k == 4:
        fills.append(("lg", q + 1))
    if q and k == LAG + 2:
        fills.append(("yT", q - 1))
    if q + 1 < NQ and k == 13:
        fills.append(("ewT", q + 1))
    return fills


def slot_order():
    order = ["w"]
    for u in range(NQ):
        order += [("cT", u), ("xT", u)]
        if u:
            order += [("MT", u - 1)]
        order += [("V", u)] + [("st", u, k) for k in range(2 * NG)]
        if u == 0:
            order += ["wo"]
    order += [("MT", NQ - 1), ("x2T", 0)]
    for tick in range(NG * (QB + 1)):
        order += last_fills(tick)
    for n in range(NQ * NB):
        order += unit_fills(n)
    order += [("yT", NQ - 1)]
    slot, bank_of, turn, used = {}, {}, {}, {}
    alternate = 0
    for n, name in enumerate(order):
        if name[0] == "st" or name[0] == "W" and name[1] < NB // 2:
            bank = STACK_BANKS[name[-1] % 4]
            alternate = 0
        else:
            bank = WORK_BANKS[alternate % 2]
            alternate += 1
        slot[name], bank_of[name], turn[name] = n, bank, used.get(bank, 0)
        used[bank] = used.get(bank, 0) + 1
    return slot, bank_of, turn


STACKS = [(0, 0), (0, 1), (1, 0), (1, 1), (1, 2), (1, 3), (0, 2), (0, 3)]
NS = len(STACKS)


def program(nc, x, ctx_in, mask, Wq, Wk, Wv, Wo, wg, w1, w3, w2, consts, out):
    slot, bank_of, turn = slot_order()
    with ExitStack() as stack:
        def sb(name, shape, dt=F32):
            return stack.enter_context(nc.sbuf_tensor(name, shape, dt))

        def sem(name):
            return stack.enter_context(nc.semaphore(name))

        cst = sb("cst", [P, C_N])
        ident = cst[:, C_ID:C_ID + P]
        x_all = sb("x_all", [P, B, D])
        ctx_all = sb("ctx_all", [P, B, D])
        mask_i = sb("mask_i", [P, T], I32)
        keep = sb("keep", [P, 2, T])
        nokeep = sb("nokeep", [P, 2, T], F32R)
        w_nat = sb("w_nat", [P, 4, D])
        wg_nat = sb("wg_nat", [P, D])
        w_hi = sb("w_hi", [P, 2, D], F32R)
        w_lo = sb("w_lo", [P, 2, D], F32R)
        ws_hi = sb("ws_hi", [P, 2, NG, P], F32R)
        ws_lo = sb("ws_lo", [P, 2, NG, P], F32R)
        wvT = sb("wvT", [P, D])
        wo_s = sb("wo_s", [P, D])
        wg_hi = sb("wg_hi", [P, E], F32R)
        wg_lo = sb("wg_lo", [P, E], F32R)
        bias_w = sb("bias_w", [P, P], F32R)
        ones_b = sb("ones_b", [P, QB, P], F32R)
        stats = sb("stats", [P, QB, 6])
        mv = sb("mv", [P, 2 * NQ, QB, 2])
        ve = sb("ve", [P, QB])
        rstd = sb("rstd", [P, 2 * NQ, QB])
        halves = sb("halves", [P, QB])
        xn = sb("xn", [P, QB, D])
        x_hi = sb("x_hi", [P, T], F32R)
        x_lo = sb("x_lo", [P, T], F32R)
        cT = sb("cT", [P, T])
        ck = sb("ck", [P, T])
        ck_hi = sb("ck_hi", [P, T], F32R)
        ck_lo = sb("ck_lo", [P, T], F32R)
        st_hi = sb("st_hi", [P, SH, T], F32R)
        st = sb("st", [P, 2, 2, NG, T], F32R)
        bd = sb("bd", [P, 6, NG * NJ * P], F32R)
        m_neg = sb("m_neg", [P, QB * H])
        m_hi = sb("m_hi", [P, QB * H], F32R)
        m_hl = sb("m_hl", [P, 2, QB * H])
        m_bd = sb("m_bd", [P, H, P], F32R)
        big = sb("big", [P, 4, 2048])
        oT = w_nat[:, :, :].rearrange("p (k a) d -> p k (a d)", k=2)
        rz = sb("rz", [P, H])
        on = sb("on", [P, P])
        onT = sb("onT", [P, P])
        lg = sb("lg", [P, QB, E])
        lsum = sb("lsum", [P, QB])
        sel = sb("sel", [P, QB, E])
        dif = sb("dif", [P, QB, E])
        rank = sb("rank", [P, QB, E])
        th = sb("th", [P, QB, E])
        ew = sb("ew", [P, QB, E])
        ew_hi = sb("ew_hi", [P, QB, E], F32R)
        ew_p = sb("ew_p", [P, QB, P])
        raw13 = sb("raw13", [P, 2, NB * P])

        prob = [big[:, k, :].rearrange("p (h q) -> p h q", h=H) for k in range(2)]
        va = [big[:, 2 + k, 0:QB * H * R].rearrange("p (m r) -> p m r", r=R) for k in range(2)]

        def bd_slot(k, n):
            return bd[:, 3 * (1 - k) + n % 3, :].rearrange("p (g j q) -> p g j q", g=NG, j=NJ)

        wt = bd[:, :, :].rearrange("p w (k c) -> p w k c", k=NB)
        w3_lo = st[:, 0, 1, :, :].rearrange("p g (m c) -> p (g m) c", c=P)
        wt_hi = [wt[:, 0], wt[:, 2], wt[:, 4]]
        wt_lo = [wt[:, 1], w3_lo, wt[:, 5]]
        raw = [raw13[:, 0, :], raw13[:, 1, :], ctx_all[:, :, :].rearrange("p b d -> p (b d)")]
        sel_e = nokeep[:, :, :].rearrange("p a (e c) -> p (a e) c", c=P)
        wo_p = on
        y_sb = cT
        o_sb = ck[:, :].rearrange("p (b d) -> p b d", b=QB)
        gt, eq = (keep[:, 0, k * QB * E * E:(k + 1) * QB * E * E].rearrange("p (b e f) -> p b e f", b=QB, e=E) for k in range(2))
        ewT = [x_hi, x_lo]
        flat = st[:, :, :, :, :].rearrange("p a b g t -> p (a b g) t")
        x2_hi = [flat[:, k, :] for k in range(2)]
        x2_lo = [flat[:, 2 + k, :] for k in range(2)]
        free = [flat[:, 8 + k, :] for k in range(8)] + [m_bd[:, 4 * k:4 * (k + 1), :].rearrange("p a c -> p (a c)") for k in range(4)]
        g_hi, g_lo = free[0:RH], free[RH:2 * RH]
        work = big[:, :, :].rearrange("p a (b t) -> p (a b) t", t=T)
        sil = [work[:, k, :] for k in range(3)]
        silw = [work[:, 3 + k, :] for k in range(3)]
        gg = [work[:, 6 + k, :] for k in range(3)]
        ewb = [work[:, 9 + k, :] for k in range(3)]

        bank = [stack.enter_context(nc.psum_tensor(f"bank{k}", [P, 512], F32)) for k in range(8)]

        def work_bank(name):
            return bank[bank_of[name]]

        s1 = [bank[0], bank[1]]
        s2 = [bank[2], bank[3]]
        ob = [bank[4], bank[5]]
        h1 = [bank[0], bank[1]]
        h3 = [bank[2], bank[3]]
        eb, yb = bank[4], bank[5]

        in_c, in_w, in_wo, in_wg, in_w13, in_w2 = sem("in_c"), sem("in_w"), sem("in_wo"), sem("in_wg"), sem("in_w13"), sem("in_w2")
        in_x = [sem(f"in_x{k}") for k in range(NQ)]
        in_ctx = [sem(f"in_ctx{k}") for k in range(NQ)]
        in_mask = [sem(f"in_mask{k}") for k in range(NQ)]
        out_done = sem("out_done")
        work_full = sem("work_full")
        work_taken = {k: sem(f"work_taken{k}") for k in STACK_BANKS}
        dve_done = sem("dve_done")
        pool_done = sem("pool_done")
        wT_hi_ready = sem("wT_hi_ready")
        wo_p_ready = sem("wo_p_ready")
        ws_cleared, ws_ready = sem("ws_cleared"), sem("ws_ready")
        va_cleared = sem("va_cleared")
        setup_ready = sem("setup_ready")
        sel_ready = sem("sel_ready")
        mask_ready = sem("mask_ready")
        var_ready = sem("var_ready")
        rstd_ready = sem("rstd_ready")
        xn_ready = sem("xn_ready")
        xhi_ready = sem("xhi_ready")
        ck_ready = sem("ck_ready")
        ckhi_ready, cklo_ready = sem("ckhi_ready"), sem("cklo_ready")
        sthi_ready = sem("sthi_ready")
        bd_cleared = sem("bd_cleared")
        kbd_ready = [sem(f"kbd_ready{k}") for k in range(3)]
        qbd_ready = [sem(f"qbd_ready{k}") for k in range(3)]
        s1_full, max_done = sem("s1_full"), sem("max_done")
        mhl_ready = sem("mhl_ready")
        s2_full, prob_ready = sem("s2_full"), sem("prob_ready")
        o_full, oT_ready = sem("o_full"), sem("oT_ready")
        oq_full, on_ready = sem("oq_full"), sem("on_ready")
        on_full, onT_ready = sem("on_full"), sem("onT_ready")
        y_full, x2_done = sem("y_full"), sem("x2_done")
        whi_ready = sem("whi_ready")
        x2hi_ready = sem("x2hi_ready")
        dif_ready, th_ready, ewp_ready = sem("dif_ready"), sem("th_ready"), sem("ewp_ready")
        eb_full, ewb_ready = sem("eb_full"), sem("ewb_ready")
        h1_full, h3_full = sem("h1_full"), sem("h3_full")
        sil_ready, silw_ready, gg_ready = sem("sil_ready"), sem("silw_ready"), sem("gg_ready")
        ghi_ready, glo_ready = sem("ghi_ready"), sem("glo_ready")
        down_done = sem("down_done")
        ysb_ready = sem("ysb_ready")

        def into_sbuf(name):
            return work_taken[bank_of[name]]

        def taken(engine, name):
            engine.wait_ge(into_sbuf(name), turn[name] + 1)

        def stacks_in(engine, u, is_k):
            for k, (kind, _) in enumerate(STACKS):
                if kind == is_k:
                    taken(engine, ("st", u, k))

        def diagonal_in(engine, k, n):
            engine.wait_ge((kbd_ready if k else qbd_ready)[n % 3], 16 * NJ * (n // 3 + 1))

        x_d = x.rearrange("(u b) s d -> u s b d", b=QB)
        ctx_d = ctx_in.rearrange("(u b) s d -> u s b d", b=QB)
        out_d = out.rearrange("(u b) s d -> u s b d", b=QB)
        mask_d = mask.rearrange("(u b) s -> u (b s)", b=QB)

        def stack_columns(ws):
            heads = ws[:, :, :, :].rearrange("p k g (j r) -> p (k g j) r", j=NJ)
            return heads[:, :, 0:3 * HD].rearrange("p h (t d) -> p h t d", t=3)

        def three_times(w):
            return w[:, :, :].rearrange("p k (h d) -> p (k h) d", d=HD).unsqueeze(2).to_broadcast([P, 2 * H, 3, HD])

        block = stack.enter_context(nc.Block())

        @block.sync
        def _(sp):
            def load(u):
                sp.dma_start(x_all[:, QB * u:QB * (u + 1), :], x_d[u]).then_inc(in_x[u], 16)
                sp.dma_start(ctx_all[:, QB * u:QB * (u + 1), :], ctx_d[u]).then_inc(in_ctx[u], 16)

            sp.dma_start(x_all[:, 0:QB, :], x_d[0]).then_inc(in_x[0], 16)
            for k, w in enumerate((Wq, Wk, Wv)):
                sp.dma_start(w_nat[:, k, :], w).then_inc(in_w, 16)
            sp.wait_ge(in_ctx[0], 16)
            for u in range(1, NQ):
                load(u)
            for k, w in enumerate((w1, w3)):
                sp.dma_start(raw[k].rearrange("p (k h) -> p k h", k=NB),
                             w.rearrange("e (c p) h -> p (e c) h", p=P)).then_inc(in_w13, 16)

            def block_diagonal(k, n):
                u, b = divmod(n, QB)
                stacks_in(sp, u, k)
                if n >= 3:
                    sp.wait_ge(s1_full if k else s2_full, NG * (n - 2))
                else:
                    sp.wait_ge(bd_cleared, 3 if k else 6)
                for j in range(NJ):
                    rows = slice(R * j, R * (j + 1))
                    sp.dma_start(bd_slot(k, n)[rows, :, j, :].bitcast(F32), st[rows, u % 2, k, :, b * S:(b + 1) * S].bitcast(F32)
                                 ).then_inc((kbd_ready if k else qbd_ready)[n % 3], 16)

            for u in range(NQ + 1):
                if u == NQ:
                    sp.wait_ge(work_full, slot["cT", NQ - 1] + 1)
                    sp.dma_start(raw[2].rearrange("p (e i) -> p e i", e=E), w2.rearrange("e h i -> h e i")).then_inc(in_w2, 16)
                for b in range(QB):
                    if u < NQ:
                        block_diagonal(1, QB * u + b)
                    if u >= 1 and b < 2:
                        block_diagonal(0, QB * (u - 1) + 2 + b)
                if u < NQ:
                    block_diagonal(0, QB * u)
                    block_diagonal(0, QB * u + 1)
            for q in range(NQ):
                taken(sp, ("yT", q))
                sp.dma_start(out_d[q], o_sb).then_inc(out_done, 16)
            sp.wait_ge(out_done, 16 * NQ)

        @block.tensor
        def _(pe):
            def claim(name):
                if turn[name]:
                    pe.wait_ge(into_sbuf(name), turn[name])
                return work_bank(name)

            def split_product(o, w_parts, m_parts, extra=None):
                pairs = [(w_parts[0], m_parts[0]), (w_parts[0], m_parts[1]), (w_parts[1], m_parts[0])]
                if extra is not None:
                    pairs.append(extra)
                for k, (w, m) in enumerate(pairs):
                    last = nc.tensor.matmul(o, w, m, start=(k == 0), stop=(k == len(pairs) - 1))
                return last

            def transpose4(name, pieces):
                o = claim(name)
                for k, piece in enumerate(pieces):
                    last = nc.tensor.transpose(o[0:piece.shape[1], P * k:P * k + piece.shape[0]], piece,
                                               ident[0:piece.shape[0], 0:piece.shape[0]])
                last.then_inc(work_full, 1)

            pe.wait_ge(in_c, 16)
            pe.wait_ge(in_w, 48)
            pe.wait_ge(in_wg, 16)
            transpose4("w", [w_nat[:, 0, :], w_nat[:, 1, :], w_nat[:, 2, :], wg_nat[0:E, :]])

            def heads_by_query(n):
                pe.wait_ge(oT_ready, n + 1)
                for half in range(2):
                    last = nc.tensor.transpose(ob[n % 2][:, (2 + half) * P:(3 + half) * P], oT[:, n % 2, half * P:(half + 1) * P], ident)
                last.then_inc(oq_full, 1)

            def heads_by_dim(n):
                pe.wait_ge(on_ready, n + 1)
                nc.tensor.transpose(ob[n % 2][:, 0:P], on[:, :], ident).then_inc(on_full, 1)

            def project_out(n):
                pe.wait_ge(onT_ready, n + 1)
                nc.tensor.matmul(ob[n % 2][:, P:2 * P], onT[:, :], wo_s[:, :], start=True, stop=True).then_inc(y_full, 1)

            def fill(name):
                kind, q = name
                if kind == "W":
                    if q < 2:
                        pe.wait_ge(max_done, NG * B)
                    if q == 0:
                        pe.wait_ge(in_w13, 32)
                    if q == NB // 2:
                        pe.wait_ge(in_w2, 16)
                    transpose4(name, [raw[q // 4][:, (4 * (q % 4) + m) * P:(4 * (q % 4) + m + 1) * P] for m in range(4)])
                if kind == "x2T":
                    pe.wait_ge(xn_ready, NQ + q + 1)
                    transpose4(name, [xn[:, b, :] for b in range(QB)])
                if kind == "lg":
                    o = claim(name)
                    taken(pe, ("x2T", q))
                    for b in range(QB):
                        t = slice(b * S, (b + 1) * S)
                        last = split_product(o[:, b * E:(b + 1) * E], (x2_hi[q % 2][:, t], x2_lo[q % 2][:, t]), (wg_hi[:, :], wg_lo[:, :]))
                    last.then_inc(work_full, 1)
                if kind == "ewT":
                    pe.wait_ge(ewp_ready, q + 1)
                    transpose4(name, [ew_p[:, b, :] for b in range(QB)])
                if kind == "yT":
                    pe.wait_ge(ysb_ready, q + 1)
                    transpose4(name, [y_sb[:, b * S:(b + 1) * S] for b in range(QB)])

            def front(u):
                if u < NQ:
                    pe.wait_ge(in_ctx[u], 16)
                    transpose4(("cT", u), [ctx_all[:, QB * u + b, :] for b in range(QB)])
                if u >= 2:
                    heads_by_query(QB * (u - 1) - 1)
                if u < NQ:
                    pe.wait_ge(xn_ready, u + 1)
                    transpose4(("xT", u), [xn[:, b, :] for b in range(QB)])
                if u >= 2:
                    heads_by_dim(QB * (u - 1) - 1)
                if u >= 1:
                    pe.wait_ge(mhl_ready, u)
                    transpose4(("MT", u - 1), [m_hl[:, :, :].rearrange("p a m -> p (a m)")])
                if u == NQ:
                    fill(("x2T", 0))
                    project_out(QB * (u - 1) - 1)
                    return
                o = claim(("V", u))
                taken(pe, ("cT", u))
                if u == 0:
                    pe.wait_ge(setup_ready, 1)
                for b in range(QB):
                    last = nc.tensor.matmul(o[:, b * D:(b + 1) * D], cT[:, b * S:(b + 1) * S], wvT[:, :], start=True, stop=True)
                last.then_inc(work_full, 1)
                if u >= 2:
                    project_out(QB * (u - 1) - 1)
                for k, (is_k, g) in enumerate(STACKS):
                    o = claim(("st", u, k))
                    if k < 2 and u:
                        pe.wait_ge(max_done, NG * QB * u)
                    if k == 0:
                        taken(pe, ("xT", u))
                        if u == 0:
                            pe.wait_ge(ws_ready, 2)
                    if is_k and g == 0:
                        pe.wait_ge(cklo_ready, u + 1)
                        pe.wait_ge(mask_ready, u + 1)
                        if u == 0:
                            pe.wait_ge(setup_ready, 2)
                    parts = (ws_hi[:, is_k, g, :], ws_lo[:, is_k, g, :])
                    if is_k:
                        last = split_product(o[:, :], parts, (ck_hi[:, :], ck_lo[:, :]), (bias_w[:, :], nokeep[:, u % 2, :]))
                    else:
                        last = split_product(o[:, :], parts, (x_hi[:, :], x_lo[:, :]))
                    last.then_inc(work_full, 1)
                if u == 0:
                    pe.wait_ge(wo_p_ready, 1)
                    transpose4("wo", [wo_p[:, :]])

            def values(n, g):
                if g == 0 and n >= 2:
                    pe.wait_ge(x2_done, n - 1)
                if g == 0 and n % QB == 0:
                    taken(pe, ("V", n // QB))
                pe.wait_ge(prob_ready, NG * n + g + 1)
                half, i = g // 2, g % 2
                for j in range(NJ):
                    last = nc.tensor.matmul(ob[n % 2][R * j:R * (j + 1), half * P:(half + 1) * P],
                                            va[(n // QB) % 2][:, ((n % QB) * 4 + half * 2 + i) * NJ + j, :],
                                            prob[n % 2][:, NJ * g + j, :], start=(i == 0), stop=(i == 1),
                                            tile_position=(0, R * j))
                if g == NG - 1:
                    last.then_inc(o_full, 1)

            for u in range(NQ + 1):
                front(u)
                for b in range(QB + 1):
                    for g in range(NG):
                        if u >= 1 and b < QB:
                            n = QB * (u - 1) + b
                            k = NG * n + g
                            if g == 0:
                                diagonal_in(pe, 0, n)
                                if b == 0:
                                    taken(pe, ("MT", u - 1))
                            if k >= 2:
                                pe.wait_ge(prob_ready, k - 1)
                            nc.tensor.matmul(s2[k % 2][:, :], ones_b[:, b, :],
                                             m_bd[:, NJ * g:NJ * (g + 1), :].rearrange("p h q -> p (h q)"),
                                             start=True, stop=False)
                            nc.tensor.matmul(s2[k % 2][:, :], st[:, (u - 1) % 2, 1, g, b * S:(b + 1) * S],
                                             bd_slot(0, n)[:, g, :, :].rearrange("p j q -> p (j q)"),
                                             start=False, stop=True).then_inc(s2_full, 1)
                        if u < NQ and b >= 1:
                            n = QB * u + b - 1
                            k = NG * n + g
                            if g == 0:
                                if b == 1:
                                    stacks_in(pe, u, 0)
                                    stacks_in(pe, u, 1)
                                diagonal_in(pe, 1, n)
                            if k >= 2:
                                pe.wait_ge(max_done, k - 1)
                            nc.tensor.matmul(s1[k % 2][:, :], st[:, u % 2, 0, g, (b - 1) * S:b * S],
                                             bd_slot(1, n)[:, g, :, :].rearrange("p j q -> p (j q)"),
                                             start=True, stop=True).then_inc(s1_full, 1)
                        if u >= 1 and b >= 1:
                            values(QB * (u - 1) + b - 1, g)
                        if u >= 1 and b >= 2 and g < 3:
                            (heads_by_query, heads_by_dim, project_out)[g](QB * (u - 1) + b - 2)
                        if u == NQ:
                            for name in last_fills(NG * b + g):
                                fill(name)

            def down(n):
                q, k = divmod(n, NB)
                if k == 0:
                    if q:
                        pe.wait_ge(ysb_ready, q)
                    else:
                        pe.wait_ge(x2_done, B)
                pe.wait_ge(glo_ready, n + 1)
                for c, (w, g) in enumerate(((wt_hi, g_hi), (wt_hi, g_lo), (wt_lo, g_hi))):
                    last = nc.tensor.matmul(yb[:, :], w[2][:, k, :], g[n % RH], start=(k == 0 and c == 0), stop=(k == NB - 1 and c == 2))
                last.then_inc(down_done, 1)

            for k in range(NB // 2 - 4, 3 * NB // 4):
                taken(pe, ("W", k))
            for n in range(NQ * NB):
                q, k = divmod(n, NB)
                e = k // 2
                if n < 2:
                    pe.wait_ge(prob_ready, NG * B)
                if k % 2 == 0:
                    if k == 0:
                        taken(pe, ("ewT", q))
                    if n:
                        pe.wait_ge(ewb_ready, n // 2)
                    else:
                        pe.wait_ge(sel_ready, 1)
                        pe.wait_ge(x2_done, B - 1)
                    nc.tensor.matmul(eb[:, :], sel_e[:, e, :], ewT[q % 2][:, :], start=True, stop=True).then_inc(eb_full, 1)
                if n >= 2:
                    pe.wait_ge(sil_ready, n - 1)
                split_product(h1[n % 2][:, :], (wt_hi[0][:, k, :], wt_lo[0][:, k, :]), (x2_hi[q % 2], x2_lo[q % 2])).then_inc(h1_full, 1)
                if n >= 2:
                    pe.wait_ge(gg_ready, n - 1)
                split_product(h3[n % 2][:, :], (wt_hi[1][:, k, :], wt_lo[1][:, k, :]), (x2_hi[q % 2], x2_lo[q % 2])).then_inc(h3_full, 1)
                if n < 3:
                    (heads_by_query, heads_by_dim, project_out)[n](B - 1)
                if n >= LAG:
                    down(n - LAG)
                for name in unit_fills(n):
                    fill(name)
            for n in range(NQ * NB - LAG, NQ * NB):
                down(n)
            fill(("yT", NQ - 1))

        @block.scalar
        def _(act):
            def copy(o, i):
                return nc.scalar.activation(o, i, ACT.Copy)

            def full(name):
                act.wait_ge(work_full, slot[name] + 1)

            act.dma_start(cst[:, :], consts).then_inc(in_c, 16)
            act.dma_start(wg_nat[0:E, :], wg).then_inc(in_wg, 16)
            act.dma_start(ctx_all[:, 0:QB, :], ctx_d[0]).then_inc(in_ctx[0], 16)
            act.dma_start(w_nat[:, 3, :], Wo).then_inc(in_wo, 16)
            full("w")
            wb = work_bank("w")
            copy(w_hi[:, :, :].rearrange("p a d -> p (a d)"), wb[:, 0:2 * D]).then_inc(wT_hi_ready, 1)
            copy(wg_hi[:, :], wb[:, 3 * P:3 * P + E]).then_inc(wT_hi_ready, 1)
            act.wait_ge(wT_hi_ready, 2)
            act.wait_ge(ws_cleared, 1)
            copy(stack_columns(ws_hi), three_times(w_hi)).then_inc(ws_ready, 1)

            def take_heads(n):
                act.wait_ge(o_full, n + 1)
                if n >= 2:
                    act.wait_ge(oq_full, n - 1)
                copy(oT[:, n % 2, :], ob[n % 2][:, 0:2 * P]).then_inc(oT_ready, 1)

            def take_normalised(n):
                act.wait_ge(on_full, n + 1)
                if n:
                    act.wait_ge(y_full, n)
                copy(onT[:, :], ob[n % 2][:, 0:P]).then_inc(onT_ready, 1)

            def take_weights(k):
                full(("W", k))
                if k == NB // 2:
                    act.wait_ge(s2_full, NG * (B - 2))
                copy(wt_hi[k // 4][:, 4 * (k % 4):4 * (k % 4) + 4, :].rearrange("p k c -> p (k c)"),
                     work_bank(("W", k))[:, :]).then_inc(whi_ready, 1)

            def prepare(q):
                full(("x2T", q))
                if q >= 2:
                    act.wait_ge(h3_full, NB * (q - 1))
                copy(x2_hi[q % 2], work_bank(("x2T", q))[:, :]).then_inc(x2hi_ready, 1)

            def squash(q):
                act.wait_ge(dif_ready, q + 1)
                nc.scalar.activation(th[:, :, :], dif[:, :, :], ACT.Tanh, scale=0.5).then_inc(th_ready, 1)

            for u in range(NQ + 1):
                last_n = QB * (u - 1) - 1
                if u >= 2:
                    take_heads(last_n)
                if u < NQ:
                    full(("cT", u))
                    if u:
                        act.wait_ge(ck_ready, u)
                    copy(cT[:, :], work_bank(("cT", u))[:, :]).then_inc(into_sbuf(("cT", u)), 1)
                    full(("xT", u))
                    copy(x_hi[:, :], work_bank(("xT", u))[:, :]).then_inc(xhi_ready, 1)
                if u >= 2:
                    take_normalised(last_n)
                if u < NQ:
                    full(("V", u))
                    if u >= 2:
                        act.wait_ge(o_full, QB * (u - 1))
                    src = work_bank(("V", u))[:, :].rearrange("p (m i j d) -> p m i j d", i=2, j=NJ, d=HD)
                    dst = va[u % 2].rearrange("p (m i j) r -> p m i j r", i=2, j=NJ)
                    if u < 2:
                        act.wait_ge(va_cleared, u + 1)
                    for i in range(2):
                        last = copy(dst[:, :, i, :, HD * i:HD * (i + 1)], src[:, :, i, :, :])
                    last.then_inc(into_sbuf(("V", u)), 1)
                    act.wait_ge(ck_ready, u + 1)
                    copy(ck_hi[:, :], ck[:, :]).then_inc(ckhi_ready, 1)
                    for k, (is_k, g) in enumerate(STACKS):
                        n = NS * u + k
                        full(("st", u, k))
                        if k >= SH:
                            taken(act, ("st", u, k - SH))
                        elif u:
                            taken(act, ("st", u - 1, NS + k - SH))
                        src = work_bank(("st", u, k))[:, :]
                        if is_k:
                            i = copy(st_hi[:, n % SH, :], src)
                        else:
                            i = nc.scalar.activation(st_hi[:, n % SH, :], src, ACT.Identity, bias=cst[:, C_ONE:C_ONE + 1])
                        i.then_inc(sthi_ready, 1)
                for b in range(QB + 1 if u else 0):
                    for g in range(NG):
                        if b >= 2 and g == 0:
                            take_heads(QB * (u - 1) + b - 2)
                        if b >= 2 and g == 2:
                            take_normalised(QB * (u - 1) + b - 2)
                        if u == NQ:
                            for name in last_fills(NG * b + g - 1) if b or g else ():
                                if name[0] == "W":
                                    take_weights(name[1])
                                if name[0] == "x2T":
                                    prepare(1)
                            if (b, g) == (0, 0):
                                prepare(0)
                            if (b, g) == (2, 3):
                                squash(0)
                        if b < QB:
                            n = QB * (u - 1) + b
                            k = NG * n + g
                            act.wait_ge(s2_full, k + 1)
                            if g == 0 and n >= 2:
                                act.wait_ge(o_full, n - 1)
                            nc.scalar.activation(prob[n % 2][:, NJ * g:NJ * (g + 1), :].rearrange("p h q -> p (h q)"),
                                                 s2[k % 2][:, :], ACT.Exp, scale=SCALE).then_inc(prob_ready, 1)

            def round_hidden(n):
                act.wait_ge(gg_ready, n + 1)
                if n >= RH:
                    act.wait_ge(down_done, n - RH + 1)
                copy(g_hi[n % RH], gg[n % 3]).then_inc(ghi_ready, 1)

            def take_y(q):
                act.wait_ge(down_done, NB * (q + 1))
                if q:
                    act.wait_ge(work_full, slot["yT", q - 1] + 1)
                copy(y_sb[:, :], yb[:, :]).then_inc(ysb_ready, 1)

            take_weights(3 * NB // 4 - 1)
            take_heads(B - 1)
            for n in range(NQ * NB):
                q, k = divmod(n, NB)
                if k % 2 == 0:
                    m = n // 2
                    act.wait_ge(eb_full, m + 1)
                    if m >= 3:
                        act.wait_ge(silw_ready, 2 * (m - 2))
                    copy(ewb[m % 3], eb[:, :]).then_inc(ewb_ready, 1)
                act.wait_ge(h1_full, n + 1)
                if n >= 3:
                    act.wait_ge(silw_ready, n - 2)
                nc.scalar.activation(sil[n % 3], h1[n % 2][:, :], ACT.Silu).then_inc(sil_ready, 1)
                if n == 2:
                    take_normalised(B - 1)
                if n:
                    round_hidden(n - 1)
                if k == LAG - 1 and q:
                    take_y(q - 1)
                if k == 2 and 2 <= q + 1 < NQ:
                    prepare(q + 1)
                if k == 10 and q + 1 < NQ:
                    squash(q + 1)
            round_hidden(NQ * NB - 1)
            take_y(NQ - 1)

        @block.gpsimd
        def _(pool):
            steps = [0]

            def own(ins):
                steps[0] += 1
                ins.then_inc(pool_done, 1)
                pool.wait_ge(pool_done, steps[0])

            def load_mask(u):
                if u:
                    pool.wait_ge(mask_ready, u)
                pool.dma_start(mask_i[:, :], mask_d[u].partition_broadcast(P)).then_inc(in_mask[u], 16)

            load_mask(0)
            nc.gpsimd.memset(halves[:, :], -0.5)
            nc.gpsimd.memset(ws_hi[:, :, :, :].bitcast(F32), 0.0)
            nc.gpsimd.memset(ws_lo[:, :, :, :].bitcast(F32), 0.0).then_inc(ws_cleared, 1)

            def inverse_deviation(m):
                pool.wait_ge(var_ready, m + 1)
                own(nc.gpsimd.tensor_scalar(ve[:, :], mv[:, m, :, 1], EPS, None, ALU.add))
                nc.gpsimd.tensor_tensor(rstd[:, m, :], ve[:, :], halves[:, :], ALU.pow).then_inc(rstd_ready, 1)

            inverse_deviation(0)
            for k in (0, 1, 2):
                nc.gpsimd.memset(bd[:, k, :].bitcast(F32), 0.0).then_inc(bd_cleared, 1)

            for u in range(NQ):
                taken(pool, ("cT", u))
                pool.wait_ge(mask_ready, u + 1)
                if u:
                    pool.wait_ge(cklo_ready, u)
                nc.gpsimd.tensor_tensor(ck[:, :], cT[:, :], keep[:, u % 2, :], ALU.mult).then_inc(ck_ready, 1)
                if u == 0:
                    for k in (3, 4, 5):
                        nc.gpsimd.memset(bd[:, k, :].bitcast(F32), 0.0).then_inc(bd_cleared, 1)
                if u + 1 < NQ:
                    load_mask(u + 1)
                    inverse_deviation(u + 1)

            pool.wait_ge(work_full, slot["st", NQ - 1, NS - 1] + 1)
            nc.gpsimd.tensor_copy(sel_e, cst[:, C_EXP:C_EXP + E].unsqueeze(2).to_broadcast([P, E, P])).then_inc(sel_ready, 1)
            inverse_deviation(NQ)
            inverse_deviation(NQ + 1)
            inverse_deviation(NQ + 2)
            for n in range(NQ * NB):
                q, k = divmod(n, NB)
                pool.wait_ge(sil_ready, n + 1)
                pool.wait_ge(ewb_ready, n // 2 + 1)
                if n >= 3:
                    pool.wait_ge(gg_ready, n - 2)
                nc.gpsimd.tensor_tensor(silw[n % 3], sil[n % 3], ewb[(n // 2) % 3], ALU.mult).then_inc(silw_ready, 1)
                if n == 7:
                    inverse_deviation(2 * NQ - 1)

        @block.vector
        def _(dve):
            steps = [0]

            def mark(ins):
                steps[0] += 1
                ins.then_inc(dve_done, 1)
                return steps[0]

            def own(ins):
                dve.wait_ge(dve_done, mark(ins))

            def full(name):
                dve.wait_ge(work_full, slot[name] + 1)

            def statistics(n0, m):
                for b in range(QB):
                    last = mark(nc.vector.bn_stats(stats[:, b, :], x_all[:, n0 + b, :]))
                dve.wait_ge(dve_done, last)
                for b in range(QB):
                    ins = nc.vector.bn_aggr(mv[:, m, b, :], stats[:, b, :])
                    last = mark(ins) if b < QB - 1 else last
                ins.then_inc(var_ready, 1)

            def normalise(n0, m):
                dve.wait_ge(rstd_ready, m + 1)
                for b in range(QB):
                    last = nc.vector.tensor_scalar(xn[:, b, :], x_all[:, n0 + b, :], mv[:, m, b, 0:1], rstd[:, m, b:b + 1],
                                                   ALU.subtract, ALU.mult)
                last.then_inc(xn_ready, 1)

            def masks(u):
                dve.wait_ge(in_mask[u], 16)
                if u >= 2:
                    dve.wait_ge(work_full, slot["st", u - 2, NS - 1] + 1)
                    dve.wait_ge(ck_ready, u - 1)
                own(nc.vector.tensor_scalar(nokeep[:, u % 2, :], mask_i[:, :], 0, None, ALU.is_equal))
                nc.vector.tensor_scalar(keep[:, u % 2, :], nokeep[:, u % 2, :].bitcast(F32), -1.0, 1.0, ALU.mult, ALU.add
                                        ).then_inc(mask_ready, 1)

            def clear_values(k):
                own(nc.vector.memset(va[k][:, :, :], 0.0))
                v = va[k].rearrange("p (m i j) r -> p m i j r", i=2, j=NJ)
                nc.vector.memset(v[:, :, 0, :, 16:17], 1.0)
                nc.vector.memset(v[:, :, 1, :, 17:18], 1.0).then_inc(va_cleared, 1)

            clear_values(0)
            dve.wait_ge(in_x[0], 16)
            statistics(0, 0)
            full("w")
            wb = work_bank("w")
            dve.wait_ge(wT_hi_ready, 2)
            nc.vector.tensor_copy(wvT[:, :], wb[:, 2 * P:3 * P]).then_inc(setup_ready, 1)
            nc.vector.tensor_tensor(wg_lo[:, :], wb[:, 3 * P:3 * P + E], wg_hi[:, :].bitcast(F32), ALU.subtract)
            nc.vector.tensor_tensor(w_lo[:, :, :].rearrange("p a d -> p (a d)"), wb[:, 0:2 * D],
                                    w_hi[:, :, :].rearrange("p a d -> p (a d)").bitcast(F32), ALU.subtract).then_inc(into_sbuf("w"), 1)
            normalise(0, 0)
            taken(dve, "w")
            dve.wait_ge(ws_cleared, 1)
            nc.vector.tensor_copy(stack_columns(ws_lo), three_times(w_lo)).then_inc(ws_ready, 1)
            masks(0)
            nc.vector.tensor_copy(bias_w[:, :], cst[:, C_BIAS:C_BIAS + P])
            nc.vector.tensor_copy(ones_b[:, :, :], cst[:, C_BATCH:C_BATCH + QB].unsqueeze(2).to_broadcast([P, QB, P])
                                  ).then_inc(setup_ready, 1)

            def take_projection(n):
                dve.wait_ge(y_full, n + 1)
                nc.vector.tensor_tensor(x_all[:, n, :], ob[n % 2][:, P:2 * P], x_all[:, n, :], ALU.add).then_inc(x2_done, 1)

            def normalise_heads(n):
                dve.wait_ge(oq_full, n + 1)
                heads = ob[n % 2][:, 2 * P:4 * P].rearrange("p (m r) -> p m r", r=R)
                own(nc.vector.reciprocal(rz[:, :].rearrange("p (m i) -> p m i", i=2), heads[:, :, 16:18]))
                if n:
                    dve.wait_ge(on_full, n)
                nc.vector.tensor_tensor(on[:, :].rearrange("p (m i d) -> p m i d", i=2, d=HD),
                                        heads[:, :, 0:16].rearrange("p m (i d) -> p m i d", i=2),
                                        rz[:, :].rearrange("p (m i) -> p m i", i=2).unsqueeze(3).to_broadcast([P, 8, 2, HD]),
                                        ALU.mult).then_inc(on_ready, 1)

            def round_maxima():
                own(nc.vector.tensor_copy(m_hi[:, :], m_neg[:, :]))
                nc.vector.tensor_copy(m_hl[:, 0, :], m_hi[:, :].bitcast(F32))
                nc.vector.tensor_tensor(m_hl[:, 1, :], m_neg[:, :], m_hi[:, :].bitcast(F32), ALU.subtract).then_inc(mhl_ready, 1)

            def second_statistics(q):
                dve.wait_ge(x2_done, QB * (q + 1))
                statistics(QB * q, NQ + q)

            def split_x2(q):
                full(("x2T", q))
                dve.wait_ge(x2hi_ready, q + 1)
                if q >= 2:
                    dve.wait_ge(h3_full, NB * (q - 1))
                nc.vector.tensor_tensor(x2_lo[q % 2], work_bank(("x2T", q))[:, :], x2_hi[q % 2].bitcast(F32),
                                        ALU.subtract).then_inc(into_sbuf(("x2T", q)), 1)

            def routing_step(q, k):
                other = lg[:, :, :].unsqueeze(2).to_broadcast([P, QB, E, E])
                this = lg[:, :, :].unsqueeze(3).to_broadcast([P, QB, E, E])
                lower = cst[:, C_LOW:C_LOW + E * E].rearrange("p (e f) -> p e f", e=E)
                if k == 0:
                    full(("lg", q))
                    nc.vector.tensor_copy(lg[:, :, :].rearrange("p b e -> p (b e)"),
                                          work_bank(("lg", q))[:, 0:QB * E]).then_inc(into_sbuf(("lg", q)), 1)
                    taken(dve, ("lg", q))
                if k < 2:
                    for b in (2 * k, 2 * k + 1):
                        own(nc.vector.tensor_tensor(eq[:, b], other[:, b], this[:, b], ALU.is_equal))
                        nc.vector.tensor_tensor(gt[:, b], other[:, b], this[:, b], ALU.is_gt)
                        last = mark(nc.vector.tensor_tensor(eq[:, b], eq[:, b], lower, ALU.mult))
                    dve.wait_ge(dve_done, last)
                if k == 2:
                    own(nc.vector.tensor_tensor(gt, gt, eq, ALU.add))
                    own(nc.vector.tensor_reduce(rank[:, :, :], gt, X, ALU.add))
                if k == 3:
                    own(nc.vector.tensor_scalar(sel[:, :, :], rank[:, :, :], 2.0, None, ALU.is_lt))
                    own(nc.vector.tensor_tensor(ew[:, :, :], sel[:, :, :], lg[:, :, :], ALU.mult))
                    own(nc.vector.tensor_reduce(lsum[:, :], ew[:, :, :], X, ALU.add))
                    nc.vector.scalar_tensor_tensor(dif[:, :, :], lg[:, :, :], 2.0, lsum[:, :].unsqueeze(2).to_broadcast([P, QB, E]),
                                                   ALU.mult, ALU.subtract).then_inc(dif_ready, 1)
                if k == 4:
                    dve.wait_ge(th_ready, q + 1)
                    own(nc.vector.tensor_scalar(ew[:, :, :], th[:, :, :], 0.5, 0.5, ALU.mult, ALU.add))
                    own(nc.vector.tensor_tensor(ew[:, :, :], ew[:, :, :], sel[:, :, :], ALU.mult))
                if k == 5:
                    own(nc.vector.tensor_copy(ew_hi[:, :, :], ew[:, :, :]))
                    nc.vector.tensor_copy(ew_p[:, :, 0:E], ew_hi[:, :, :].bitcast(F32))
                    nc.vector.tensor_tensor(ew_p[:, :, E:2 * E], ew[:, :, :], ew_hi[:, :, :].bitcast(F32),
                                            ALU.subtract).then_inc(ewp_ready, 1)

            def take_weights(q):
                full(("ewT", q))
                if q >= 2:
                    dve.wait_ge(eb_full, E * (q - 1))
                nc.vector.tensor_copy(ewT[q % 2][:, :], work_bank(("ewT", q))[:, :]).then_inc(into_sbuf(("ewT", q)), 1)

            def finish(q):
                full(("yT", q))
                if q:
                    dve.wait_ge(out_done, 16 * q)
                nc.vector.tensor_tensor(o_sb.rearrange("p b d -> p (b d)"), work_bank(("yT", q))[:, :],
                                        x_all[:, QB * q:QB * (q + 1), :].rearrange("p b d -> p (b d)"),
                                        ALU.add).then_inc(into_sbuf(("yT", q)), 1)

            def rest_of_weights(k):
                full(("W", k))
                dve.wait_ge(whi_ready, k + 1)
                if k == NB // 2:
                    dve.wait_ge(s2_full, NG * (B - 1))
                piece = slice(4 * (k % 4), 4 * (k % 4) + 4)
                nc.vector.tensor_tensor(wt_lo[k // 4][:, piece, :].rearrange("p k c -> p (k c)"), work_bank(("W", k))[:, :],
                                        wt_hi[k // 4][:, piece, :].rearrange("p k c -> p (k c)").bitcast(F32),
                                        ALU.subtract).then_inc(into_sbuf(("W", k)), 1)

            for u in range(NQ + 1):
                if u >= 2:
                    normalise_heads(QB * (u - 1) - 1)
                if u < NQ:
                    full(("xT", u))
                    dve.wait_ge(xhi_ready, u + 1)
                    if u:
                        dve.wait_ge(work_full, slot["st", u - 1, 2 * NG - 1] + 1)
                    nc.vector.tensor_tensor(x_lo[:, :], work_bank(("xT", u))[:, :], x_hi[:, :].bitcast(F32),
                                            ALU.subtract).then_inc(into_sbuf(("xT", u)), 1)
                if u >= 1:
                    full(("MT", u - 1))
                    if u >= 2:
                        dve.wait_ge(s2_full, NG * QB * (u - 1))
                    mt = work_bank(("MT", u - 1))[:, 0:P]
                    nc.vector.tensor_tensor(m_bd[:, :, :], mt.unsqueeze(1).to_broadcast([P, H, P]),
                                            cst[:, C_HEAD:C_HEAD + H].unsqueeze(2).to_broadcast([P, H, P]),
                                            ALU.mult).then_inc(into_sbuf(("MT", u - 1)), 1)
                if u >= 2:
                    take_projection(QB * (u - 1) - 1)
                if u == NQ:
                    split_x2(0)
                if u == 0:
                    dve.wait_ge(in_wo, 16)
                    for half in range(2):
                        cols = slice(half * D // 2, (half + 1) * D // 2)
                        last = nc.vector.tensor_copy(wo_p[:, cols].rearrange("p (j i d) -> p j i d", i=2, d=HD),
                                                     w_nat[:, 3, cols].rearrange("p (i j d) -> p j i d", i=2, d=HD))
                    last.then_inc(wo_p_ready, 1)
                if u < NQ:
                    dve.wait_ge(ckhi_ready, u + 1)
                    nc.vector.tensor_tensor(ck_lo[:, :], ck[:, :], ck_hi[:, :].bitcast(F32), ALU.subtract).then_inc(cklo_ready, 1)
                    if u >= 2:
                        dve.wait_ge(s1_full, NG * QB * (u - 1))
                        dve.wait_ge(s2_full, NG * QB * (u - 1))
                        for n in range(QB * (u - 1) - 3, QB * (u - 1)):
                            diagonal_in(dve, 1, n)
                            diagonal_in(dve, 0, n)
                    for k, (is_k, g) in enumerate(STACKS):
                        n = NS * u + k
                        full(("st", u, k))
                        dve.wait_ge(sthi_ready, n + 1)
                        nc.vector.scalar_tensor_tensor(
                            st[:, u % 2, is_k, g, :], st_hi[:, n % SH, :].bitcast(F32),
                            cst[:, (C_CK if is_k else C_CQ):(C_CK if is_k else C_CQ) + 1],
                            work_bank(("st", u, k))[:, :], ALU.mult, ALU.add).then_inc(into_sbuf(("st", u, k)), 1)
                if u == 0:
                    full("wo")
                    nc.vector.tensor_copy(wo_s[:, :], work_bank("wo")[:, 0:D]).then_inc(into_sbuf("wo"), 1)
                    nc.vector.memset(ew_p[:, :, :], 0.0)
                    clear_values(1)
                for b in range(QB + 1):
                    for g in range(NG):
                        if u >= 1 and b >= 2 and g == 1:
                            normalise_heads(QB * (u - 1) + b - 2)
                        if u >= 1 and b >= 2 and g == 3:
                            take_projection(QB * (u - 1) + b - 2)
                        if u == NQ:
                            tick = NG * b + g
                            for name in last_fills(tick - 1) if tick else ():
                                if name[0] == "W":
                                    rest_of_weights(name[1])
                                if name[0] == "x2T":
                                    split_x2(1)
                            if tick == 1:
                                normalise(QB, NQ + 1)
                            if tick == 10:
                                second_statistics(2)
                            if 2 <= tick < 10 and tick % 2 == 0:
                                routing_step(0, tick // 2 - 1)
                            if tick in (11, 12):
                                routing_step(0, tick - 7)
                            if tick == 14:
                                take_weights(0)
                        if u < NQ and b >= 1:
                            k = NG * (QB * u + b - 1) + g
                            dve.wait_ge(s1_full, k + 1)
                            nc.vector.tensor_reduce(m_neg[:, H * (b - 1) + NJ * g:H * (b - 1) + NJ * (g + 1)],
                                                    s1[k % 2][:, :].rearrange("p (j q) -> p j q", j=NJ), X, ALU.max,
                                                    negate=True).then_inc(max_done, 1)
                    if u < NQ and b == QB:
                        dve.wait_ge(max_done, NG * QB * (u + 1))
                        round_maxima()
                    if u + 1 < NQ:
                        if b == 1:
                            dve.wait_ge(in_x[u + 1], 16)
                            statistics(QB * (u + 1), u + 1)
                        if b == 2:
                            normalise(QB * (u + 1), u + 1)
                            masks(u + 1)
                    elif u + 1 == NQ:
                        if b == 1:
                            second_statistics(0)
                        if b == 2:
                            normalise(0, NQ)
                        if b == 4:
                            second_statistics(1)
            def hidden_rest(n):
                dve.wait_ge(ghi_ready, n + 1)
                dve.wait_ge(gg_ready, n + 1)
                if n >= RH:
                    dve.wait_ge(down_done, n - RH + 1)
                nc.vector.tensor_tensor(g_lo[n % RH], gg[n % 3], g_hi[n % RH].bitcast(F32), ALU.subtract).then_inc(glo_ready, 1)

            rest_of_weights(3 * NB // 4 - 1)
            for n in range(NQ * NB):
                q, k = divmod(n, NB)
                if n == 1:
                    normalise_heads(B - 1)
                if n == 3:
                    take_projection(B - 1)
                dve.wait_ge(silw_ready, n + 1)
                dve.wait_ge(h3_full, n + 1)
                if n >= 3:
                    dve.wait_ge(glo_ready, n - 2)
                nc.vector.tensor_tensor(gg[n % 3], silw[n % 3], h3[n % 2][:, :], ALU.mult).then_inc(gg_ready, 1)
                if n:
                    hidden_rest(n - 1)
                if k == LAG + 3 and q:
                    finish(q - 1)
                if n == 6:
                    second_statistics(NQ - 1)
                if 2 <= q + 1 < NQ:
                    if k == 2:
                        split_x2(q + 1)
                if q + 2 < NQ and k == 14:
                    normalise(QB * (q + 2), NQ + q + 2)
                if q + 1 < NQ:
                    if 5 <= k < 9:
                        routing_step(q + 1, k - 5)
                    if k in (10, 11):
                        routing_step(q + 1, k - 6)
                    if k == 13:
                        take_weights(q + 1)
            hidden_rest(NQ * NB - 1)
            finish(NQ - 1)


_INS = ["x", "ctx_1024", "mask_BxS2_if1", "L0_xattn_Wq", "L0_xattn_Wk", "L0_xattn_Wv", "L0_xattn_Wo", "L0_ffn_wg",
        "L0_ffn_w1", "L0_ffn_w3", "L0_ffn_w2"]


def kernel(**inputs):
    import concourse.bacc as bacc
    from concourse.bass_utils import run_bass_kernel_spmd

    nc = bacc.Bacc("TRN2", target_bir_lowering=False, num_devices=1)
    arrays = {f"in_{name}": np.ascontiguousarray(inputs[name]) for name in _INS}
    arrays["in_patterns"] = constants()
    args = [nc.dram_tensor(name, a.shape, mybir.dt.from_np(a.dtype), kind="ExternalInput").ap() for name, a in arrays.items()]
    out = nc.dram_tensor("out", (B, S, D), F32, kind="ExternalOutput").ap()
    program(nc, *args, out)
    return run_bass_kernel_spmd(nc, [arrays], core_ids=[0]).results[0]["out"]
```

```python
from contextlib import ExitStack

import numpy as np

import concourse.bass as bass
from concourse import mybir

F32 = mybir.dt.float32
F32R = mybir.dt.float32r
I32 = mybir.dt.int32
ALU = mybir.AluOpType
ACT = mybir.ActivationFunctionType
X = mybir.AxisListType.X

P = 128
B, S, D = 16, 128, 128
H, HD = 16, 8
NG, NJ = 4, 4
R = 32
QB = 4
NQ = B // QB
T = QB * S
E, I = 8, 256
NB = E * I // P
SCALE = float(HD) ** -0.5
NEG = -1.0e9 / SCALE
EPS = 1e-5
LAG = 5
RH = 6
SH = 3


def split_constant(v):
    bits = np.float32(v).view(np.uint32)
    hi = np.uint32(bits & np.uint32(0xFFFFF000)).view(np.float32)
    return float(hi), float(np.float32(np.float32(v) - hi))


C_ID, C_CQ, C_CK, C_ONE, C_HEAD, C_BATCH, C_LOW, C_BIAS, C_N = 0, 128, 129, 130, 132, 148, 152, 216, 344


def constants():
    c = np.zeros((P, C_N), np.float32)
    p = np.arange(P)
    r = p % R
    c[:, C_ID:C_ID + P] = np.eye(P)
    c[:, C_CQ] = np.where((r >= 16) & (r < 24), -1.0, np.where((r == 24) | (r == 25), 1.0, 0.0))
    c[:, C_CK] = np.where((r >= 8) & (r < 16), -1.0, 0.0)
    c[:, C_ONE] = (r == 24) | (r == 25)
    for h in range(H):
        c[:, C_HEAD + h] = p % H == h
    for b in range(QB):
        c[:, C_BATCH + b] = (p // H) % QB == b
    for e in range(E):
        c[:, C_LOW + E * e:C_LOW + E * e + e] = 1.0
    hi, lo = split_constant(NEG)
    for j in range(NJ):
        c[0, C_BIAS + R * j + 24] = hi
        c[0, C_BIAS + R * j + 25] = lo
    return c


WORK_BANKS, STACK_BANKS = (6, 7), (0, 1, 6, 7)


LAST_FILLS = {-1: [("W", 0), ("W", 1), ("lg", 0), ("W", 2), ("W", 3)], 0: [("W", 4)], 2: [("W", 5)], 4: [("W", 6)], 6: [("W", 7)],
              8: [("ewT", 0)], 10: [("x2T", 1)], 12: [("W", 8)], 14: [("W", 9)], 15: [("W", 10)], 16: [("W", 11)]}


def last_fills(tick):
    return LAST_FILLS.get(tick, [])


def unit_fills(n):
    q, k = divmod(n, NB)
    fills = []
    if 2 <= q + 1 < NQ and k == 1:
        fills.append(("x2T", q + 1))
    if q + 1 < NQ and k == 4:
        fills.append(("lg", q + 1))
    if q and k == LAG + 2:
        fills.append(("yT", q - 1))
    if q + 1 < NQ and k == 12:
        fills.append(("ewT", q + 1))
    return fills


def slot_order():
    order = ["w", ("cT", 0), ("xT", 0)]
    for u in range(NQ):
        order += [("V", u)]
        if u:
            order += [("MT", u - 1)]
        order += [("st", u, k) for k in range(2 * NG)]
        if u == 0:
            order += ["wo"]
        order += [("cT", u + 1), ("xT", u + 1)] if u + 1 < NQ else [("x2T", 0)]
    order += [("MT", NQ - 1)]
    for tick in range(-1, NG * (QB + 1)):
        order += last_fills(tick)
    for n in range(NQ * NB):
        order += unit_fills(n)
    order += [("yT", NQ - 1)]
    slot, bank_of, turn, used = {}, {}, {}, {}
    alternate = 0
    for n, name in enumerate(order):
        if name[0] == "st" or name[0] == "W" and name[1] < NB // 2:
            bank = STACK_BANKS[name[-1] % 4]
            alternate = 0
        else:
            bank = WORK_BANKS[alternate % 2]
            alternate += 1
        slot[name], bank_of[name], turn[name] = n, bank, used.get(bank, 0)
        used[bank] = used.get(bank, 0) + 1
    return slot, bank_of, turn


STACKS = [(0, 0), (1, 0), (1, 1), (1, 2), (1, 3), (0, 1), (0, 2), (0, 3)]
NS = len(STACKS)


def program(nc, x, ctx_in, mask, Wq, Wk, Wv, Wo, wg, w1, w3, w2, consts, ew_rows, out):
    slot, bank_of, turn = slot_order()
    with ExitStack() as stack:
        def sb(name, shape, dt=F32):
            return stack.enter_context(nc.sbuf_tensor(name, shape, dt))

        def sem(name):
            return stack.enter_context(nc.semaphore(name))

        cst = sb("cst", [P, C_N])
        ident = cst[:, C_ID:C_ID + P]
        x_all = sb("x_all", [P, B, D])
        ctx_all = sb("ctx_all", [P, B, D])
        mask_i = sb("mask_i", [P, T], I32)
        keep = sb("keep", [P, 2, T])
        nokeep = sb("nokeep", [P, 2, T], F32R)
        w_nat = sb("w_nat", [P, 4, D])
        wg_nat = sb("wg_nat", [P, D])
        w_hi = sb("w_hi", [P, 2, D], F32R)
        w_lo = sb("w_lo", [P, 2, D], F32R)
        ws_hi = sb("ws_hi", [P, 2, NG, P], F32R)
        ws_lo = sb("ws_lo", [P, 2, NG, P], F32R)
        wvT = sb("wvT", [P, D])
        wo_s = sb("wo_s", [P, D])
        wg_hi = sb("wg_hi", [P, E], F32R)
        wg_lo = sb("wg_lo", [P, E], F32R)
        bias_w = sb("bias_w", [P, P], F32R)
        ones_b = sb("ones_b", [P, QB, P], F32R)
        stats = sb("stats", [P, QB, 6])
        mv = sb("mv", [P, 2 * NQ, QB, 2])
        ve = sb("ve", [P, QB])
        rstd = sb("rstd", [P, 2 * NQ, QB])
        halves = sb("halves", [P, QB])
        xn = sb("xn", [P, QB, D])
        x_hi = sb("x_hi", [P, T], F32R)
        x_lo = sb("x_lo", [P, T], F32R)
        cT = sb("cT", [P, T])
        ck = sb("ck", [P, T])
        ck_hi = sb("ck_hi", [P, T], F32R)
        ck_lo = sb("ck_lo", [P, T], F32R)
        st_hi = sb("st_hi", [P, SH, T], F32R)
        st = sb("st", [P, 2, 2, NG, T], F32R)
        bd = sb("bd", [P, 6, NG * NJ * P], F32R)
        m_neg = sb("m_neg", [P, QB * H])
        m_hi = sb("m_hi", [P, QB * H], F32R)
        m_hl = sb("m_hl", [P, 2, QB * H])
        mT = sb("mT", [P, P])
        m_bd = sb("m_bd", [P, H, P], F32R)
        unused = sb("unused", [P, 1])
        big = sb("big", [P, 4, 2048])
        oT = w_nat[:, :, :].rearrange("p (k a) d -> p k (a d)", k=2)
        rz = sb("rz", [P, H])
        on = sb("on", [P, P])
        onT = sb("onT", [P, P])
        lg = sb("lg", [P, QB, E])
        lsum = sb("lsum", [P, QB])
        sel = sb("sel", [P, QB, E])
        dif = sb("dif", [P, QB, E])
        rank = sb("rank", [P, QB, E])
        th = sb("th", [P, QB, E])
        ew = sb("ew", [P, QB, E])
        raw13 = sb("raw13", [P, 2, NB * P])

        prob = [big[:, k, :].rearrange("p (h q) -> p h q", h=H) for k in range(2)]
        va = [big[:, 2 + k, 0:QB * H * R].rearrange("p (m r) -> p m r", r=R) for k in range(2)]

        def bd_slot(k, n):
            return bd[:, 3 * (1 - k) + n % 3, :].rearrange("p (g j q) -> p g j q", g=NG, j=NJ)

        wt = bd[:, :, :].rearrange("p w (k c) -> p w k c", k=NB)
        w3_lo = st[:, 0, 1, :, :].rearrange("p g (m c) -> p (g m) c", c=P)
        wt_hi = [wt[:, 0], wt[:, 2], wt[:, 4]]
        wt_lo = [wt[:, 1], w3_lo, wt[:, 5]]
        raw = [raw13[:, 0, :], raw13[:, 1, :], ctx_all[:, :, :].rearrange("p b d -> p (b d)")]
        wo_p = on
        y_sb = cT
        o_sb = ck[:, :].rearrange("p (b d) -> p b d", b=QB)
        gt, eq = (keep[:, 0, k * QB * E * E:(k + 1) * QB * E * E].rearrange("p (b e f) -> p b e f", b=QB, e=E) for k in range(2))
        ewT = keep[0:E, 1, :]
        ewb = raw13[:, :, :].rearrange("p a (e t) -> p (a e) t", t=T)
        flat = st[:, :, :, :, :].rearrange("p a b g t -> p (a b g) t")
        x2_hi = [flat[:, k, :] for k in range(2)]
        x2_lo = [flat[:, 2 + k, :] for k in range(2)]
        free = [flat[:, 8 + k, :] for k in range(8)] + [m_bd[:, 4 * k:4 * (k + 1), :].rearrange("p a c -> p (a c)") for k in range(4)]
        g_hi, g_lo = free[0:RH], free[RH:2 * RH]
        work = big[:, :, :].rearrange("p a (b t) -> p (a b) t", t=T)
        sil = [work[:, k, :] for k in range(3)]
        silw = [work[:, 3 + k, :] for k in range(3)]
        gg = [work[:, 6 + k, :] for k in range(3)]

        bank = [stack.enter_context(nc.psum_tensor(f"bank{k}", [P, 512], F32)) for k in range(8)]

        def work_bank(name):
            return bank[bank_of[name]]

        s1 = bank[0:4]
        s2 = [bank[2], bank[3]]
        ob = [bank[4], bank[5]]

        def s1_ring(u):
            return 2 if u else 4

        h1 = [bank[0], bank[1]]
        h3 = [bank[2], bank[3]]
        yb = [bank[5], bank[4]]

        in_c, in_w, in_wo, in_wg, in_w13, in_w2 = sem("in_c"), sem("in_w"), sem("in_wo"), sem("in_wg"), sem("in_w13"), sem("in_w2")
        in_x = [sem(f"in_x{k}") for k in range(NQ)]
        in_ctx = [sem(f"in_ctx{k}") for k in range(NQ)]
        in_mask = [sem(f"in_mask{k}") for k in range(NQ)]
        out_done = sem("out_done")
        rows_out = sem("rows_out")
        work_full = sem("work_full")
        work_taken = {k: sem(f"work_taken{k}") for k in STACK_BANKS}
        dve_done = sem("dve_done")
        pool_done = sem("pool_done")
        wT_hi_ready = sem("wT_hi_ready")
        wo_p_ready = sem("wo_p_ready")
        ws_cleared, ws_ready = sem("ws_cleared"), sem("ws_ready")
        va_cleared = sem("va_cleared")
        setup_ready = sem("setup_ready")
        mask_ready = sem("mask_ready")
        var_ready = sem("var_ready")
        rstd_ready = sem("rstd_ready")
        xn_ready = sem("xn_ready")
        xhi_ready = sem("xhi_ready")
        ck_ready = sem("ck_ready")
        ckhi_ready, cklo_ready = sem("ckhi_ready"), sem("cklo_ready")
        sthi_ready = sem("sthi_ready")
        bd_cleared = sem("bd_cleared")
        kbd_ready = [sem(f"kbd_ready{k}") for k in range(3)]
        qbd_ready = [sem(f"qbd_ready{k}") for k in range(3)]
        s1_full, max_done = sem("s1_full"), sem("max_done")
        mhl_ready = sem("mhl_ready")
        mbd_ready = sem("mbd_ready")
        s2_full, prob_ready = sem("s2_full"), sem("prob_ready")
        o_full, oT_ready = sem("o_full"), sem("oT_ready")
        oq_full, on_ready = sem("oq_full"), sem("on_ready")
        on_full, onT_ready = sem("on_full"), sem("onT_ready")
        y_full, x2_done = sem("y_full"), sem("x2_done")
        whi_ready = sem("whi_ready")
        x2hi_ready = sem("x2hi_ready")
        dif_ready, th_ready, ew_ready = sem("dif_ready"), sem("th_ready"), sem("ew_ready")
        in_ewb = [sem(f"in_ewb{e}") for e in range(E)]
        h1_full, h3_full = sem("h1_full"), sem("h3_full")
        sil_ready, silw_ready, gg_ready = sem("sil_ready"), sem("silw_ready"), sem("gg_ready")
        ghi_ready, glo_ready = sem("ghi_ready"), sem("glo_ready")
        down_done = sem("down_done")
        ysb_ready = sem("ysb_ready")

        def into_sbuf(name):
            return work_taken[bank_of[name]]

        def taken(engine, name):
            engine.wait_ge(into_sbuf(name), turn[name] + 1)

        def stacks_in(engine, u, is_k):
            for k, (kind, _) in enumerate(STACKS):
                if kind == is_k:
                    taken(engine, ("st", u, k))

        def diagonal_in(engine, k, n):
            engine.wait_ge((kbd_ready if k else qbd_ready)[n % 3], 16 * NJ * (n // 3 + 1))

        x_d = x.rearrange("(u b) s d -> u s b d", b=QB)
        ctx_d = ctx_in.rearrange("(u b) s d -> u s b d", b=QB)
        out_d = out.rearrange("(u b) s d -> u s b d", b=QB)
        mask_d = mask.rearrange("(u b) s -> u (b s)", b=QB)

        def stack_columns(ws):
            heads = ws[:, :, :, :].rearrange("p k g (j r) -> p (k g j) r", j=NJ)
            return heads[:, :, 0:3 * HD].rearrange("p h (t d) -> p h t d", t=3)

        def three_times(w):
            return w[:, :, :].rearrange("p k (h d) -> p (k h) d", d=HD).unsqueeze(2).to_broadcast([P, 2 * H, 3, HD])

        block = stack.enter_context(nc.Block())

        @block.sync
        def _(sp):
            def load(u):
                sp.dma_start(x_all[:, QB * u:QB * (u + 1), :], x_d[u]).then_inc(in_x[u], 16)
                sp.dma_start(ctx_all[:, QB * u:QB * (u + 1), :], ctx_d[u]).then_inc(in_ctx[u], 16)

            sp.dma_start(x_all[:, 0:QB, :], x_d[0]).then_inc(in_x[0], 16)
            for k, w in enumerate((Wq, Wk, Wv)):
                sp.dma_start(w_nat[:, k, :], w).then_inc(in_w, 16)
            sp.wait_ge(in_ctx[0], 16)
            for u in range(1, NQ):
                load(u)
            for k, w in enumerate((w1, w3)):
                sp.dma_start(raw[k].rearrange("p (k h) -> p k h", k=NB),
                             w.rearrange("e (c p) h -> p (e c) h", p=P)).then_inc(in_w13, 16)

            def block_diagonal(k, n):
                u, b = divmod(n, QB)
                stacks_in(sp, u, k)
                if n >= 3:
                    sp.wait_ge(s1_full if k else s2_full, NG * (n - 2))
                else:
                    sp.wait_ge(bd_cleared, 3 if k else 6)
                for j in range(NJ):
                    rows = slice(R * j, R * (j + 1))
                    sp.dma_start(bd_slot(k, n)[rows, :, j, :].bitcast(F32), st[rows, u % 2, k, :, b * S:(b + 1) * S].bitcast(F32)
                                 ).then_inc((kbd_ready if k else qbd_ready)[n % 3], 16)

            for u in range(NQ + 1):
                if u == NQ:
                    sp.wait_ge(work_full, slot["cT", NQ - 1] + 1)
                    sp.dma_start(raw[2].rearrange("p (e i) -> p e i", e=E), w2.rearrange("e h i -> h e i")).then_inc(in_w2, 16)
                for k, b in ((1, 0), (1, 1), (1, 2), (0, 3), (1, 3)):
                    if k and u < NQ:
                        block_diagonal(1, QB * u + b)
                    if not k and u >= 1:
                        block_diagonal(0, QB * (u - 1) + b)
                if u < NQ:
                    block_diagonal(0, QB * u)
                    block_diagonal(0, QB * u + 1)
                    block_diagonal(0, QB * u + 2)

            def spread_weights(q):
                taken(sp, ("ewT", q))
                sp.dma_start(ew_rows[q], ewT).then_inc(rows_out, 16)
                sp.wait_ge(rows_out, 16 * (q + 1))
                for e in range(E):
                    if q:
                        sp.wait_ge(silw_ready, NB * (q - 1) + 2 * e + 2)
                    else:
                        sp.wait_ge(work_full, slot["W", 3 if e < E // 2 else 7] + 1)
                    sp.dma_start(ewb[:, e, :], ew_rows[q, e].partition_broadcast(P)).then_inc(in_ewb[e], 16)

            def store(q):
                taken(sp, ("yT", q))
                sp.dma_start(out_d[q], o_sb).then_inc(out_done, 16)

            spread_weights(0)
            for q in range(NQ):
                if q + 1 < NQ:
                    spread_weights(q + 1)
                store(q)
            sp.wait_ge(out_done, 16 * NQ)

        @block.tensor
        def _(pe):
            def claim(name):
                if turn[name]:
                    pe.wait_ge(into_sbuf(name), turn[name])
                return work_bank(name)

            def split_product(o, w_parts, m_parts, extra=None):
                pairs = [(w_parts[0], m_parts[0]), (w_parts[0], m_parts[1]), (w_parts[1], m_parts[0])]
                if extra is not None:
                    pairs.append(extra)
                for k, (w, m) in enumerate(pairs):
                    last = nc.tensor.matmul(o, w, m, start=(k == 0), stop=(k == len(pairs) - 1))
                return last

            def transpose4(name, pieces):
                o = claim(name)
                for k, piece in enumerate(pieces):
                    last = nc.tensor.transpose(o[0:piece.shape[1], P * k:P * k + piece.shape[0]], piece,
                                               ident[0:piece.shape[0], 0:piece.shape[0]])
                last.then_inc(work_full, 1)

            pe.wait_ge(in_c, 16)
            pe.wait_ge(in_w, 48)
            pe.wait_ge(in_wg, 16)
            transpose4("w", [w_nat[:, 0, :], w_nat[:, 1, :], w_nat[:, 2, :], wg_nat[0:E, :]])

            def heads_by_query(n):
                pe.wait_ge(oT_ready, n + 1)
                for half in range(2):
                    last = nc.tensor.transpose(ob[n % 2][:, (2 + half) * P:(3 + half) * P], oT[:, n % 2, half * P:(half + 1) * P], ident)
                last.then_inc(oq_full, 1)

            def heads_by_dim(n):
                pe.wait_ge(on_ready, n + 1)
                nc.tensor.transpose(ob[n % 2][:, 0:P], on[:, :], ident).then_inc(on_full, 1)

            def project_out(n):
                pe.wait_ge(onT_ready, n + 1)
                nc.tensor.matmul(ob[n % 2][:, P:2 * P], onT[:, :], wo_s[:, :], start=True, stop=True).then_inc(y_full, 1)

            def fill(name):
                kind, q = name
                if kind == "W":
                    if q < 2:
                        pe.wait_ge(max_done, NG * B)
                    if q == 0:
                        pe.wait_ge(in_w13, 32)
                    if q == NB // 2:
                        pe.wait_ge(in_w2, 16)
                    transpose4(name, [raw[q // 4][:, (4 * (q % 4) + m) * P:(4 * (q % 4) + m + 1) * P] for m in range(4)])
                if kind == "x2T":
                    pe.wait_ge(xn_ready, QB * (NQ + q + 1))
                    transpose4(name, [xn[:, b, :] for b in range(QB)])
                if kind == "lg":
                    o = claim(name)
                    taken(pe, ("x2T", q))
                    for b in range(QB):
                        t = slice(b * S, (b + 1) * S)
                        last = split_product(o[:, b * E:(b + 1) * E], (x2_hi[q % 2][:, t], x2_lo[q % 2][:, t]), (wg_hi[:, :], wg_lo[:, :]))
                    last.then_inc(work_full, 1)
                if kind == "ewT":
                    pe.wait_ge(ew_ready, q + 1)
                    transpose4(name, [ew[:, b, :] for b in range(QB)])
                if kind == "yT":
                    pe.wait_ge(ysb_ready, q + 1)
                    transpose4(name, [y_sb[:, b * S:(b + 1) * S] for b in range(QB)])

            def transpose_context(u):
                pe.wait_ge(in_ctx[u], 16)
                transpose4(("cT", u), [ctx_all[:, QB * u + b, :] for b in range(QB)])

            def transpose_tokens(u):
                pe.wait_ge(xn_ready, QB * (u + 1))
                transpose4(("xT", u), [xn[:, b, :] for b in range(QB)])

            def transpose_maxima(u):
                pe.wait_ge(mhl_ready, u + 1)
                transpose4(("MT", u), [m_hl[:, :, :].rearrange("p a m -> p (a m)")])

            def front(u):
                if u >= 2:
                    heads_by_query(QB * (u - 1) - 1)
                if u == NQ:
                    transpose_maxima(u - 1)
                    for name in last_fills(-1)[:2]:
                        fill(name)
                    heads_by_dim(QB * (u - 1) - 1)
                    project_out(QB * (u - 1) - 1)
                    for name in last_fills(-1)[2:]:
                        fill(name)
                    return
                o = claim(("V", u))
                taken(pe, ("cT", u))
                if u == 0:
                    pe.wait_ge(setup_ready, 1)
                for b in range(QB):
                    last = nc.tensor.matmul(o[:, b * D:(b + 1) * D], cT[:, b * S:(b + 1) * S], wvT[:, :], start=True, stop=True)
                last.then_inc(work_full, 1)
                if u >= 1:
                    transpose_maxima(u - 1)
                for k, (is_k, g) in enumerate(STACKS):
                    if k in (1, 3) and u >= 2:
                        (heads_by_dim if k == 1 else project_out)(QB * (u - 1) - 1)
                    o = claim(("st", u, k))
                    if k < 2 and u:
                        pe.wait_ge(max_done, NG * QB * u)
                    if k == 0:
                        taken(pe, ("xT", u))
                        if u == 0:
                            pe.wait_ge(ws_ready, 2)
                    if is_k and g == 0:
                        pe.wait_ge(cklo_ready, u + 1)
                        pe.wait_ge(mask_ready, u + 1)
                        if u == 0:
                            pe.wait_ge(setup_ready, 2)
                    parts = (ws_hi[:, is_k, g, :], ws_lo[:, is_k, g, :])
                    if is_k:
                        last = split_product(o[:, :], parts, (ck_hi[:, :], ck_lo[:, :]), (bias_w[:, :], nokeep[:, u % 2, :]))
                    else:
                        last = split_product(o[:, :], parts, (x_hi[:, :], x_lo[:, :]))
                    last.then_inc(work_full, 1)
                if u == 0:
                    pe.wait_ge(wo_p_ready, 1)
                    transpose4("wo", [wo_p[:, :]])

            def values(n, g):
                if g == 0 and n >= 2:
                    pe.wait_ge(x2_done, n - 1)
                if g == 0 and n % QB == 0:
                    taken(pe, ("V", n // QB))
                pe.wait_ge(prob_ready, NG * n + g + 1)
                half, i = g // 2, g % 2
                for j in range(NJ):
                    last = nc.tensor.matmul(ob[n % 2][R * j:R * (j + 1), half * P:(half + 1) * P],
                                            va[(n // QB) % 2][:, ((n % QB) * 4 + half * 2 + i) * NJ + j, :],
                                            prob[n % 2][:, NJ * g + j, :], start=(i == 0), stop=(i == 1),
                                            tile_position=(0, R * j))
                if g == NG - 1:
                    last.then_inc(o_full, 1)

            transpose_context(0)
            transpose_tokens(0)
            for u in range(NQ + 1):
                front(u)
                for b in range(QB + 1):
                    for g in range(NG):
                        if u >= 1 and b < QB:
                            n = QB * (u - 1) + b
                            k = NG * n + g
                            if g == 0:
                                diagonal_in(pe, 0, n)
                            if k >= 2:
                                pe.wait_ge(prob_ready, k - 1)
                            if b == 0:
                                pe.wait_ge(mbd_ready, NG * (u - 1) + g + 1)
                            nc.tensor.matmul(s2[k % 2][:, :], ones_b[:, b, :],
                                             m_bd[:, NJ * g:NJ * (g + 1), :].rearrange("p h q -> p (h q)"),
                                             start=True, stop=False)
                            nc.tensor.matmul(s2[k % 2][:, :], st[:, (u - 1) % 2, 1, g, b * S:(b + 1) * S],
                                             bd_slot(0, n)[:, g, :, :].rearrange("p j q -> p (j q)"),
                                             start=False, stop=True).then_inc(s2_full, 1)
                        if u < NQ and b >= 1:
                            n = QB * u + b - 1
                            k = NG * n + g
                            if g == 0:
                                if b == 1:
                                    stacks_in(pe, u, 0)
                                    stacks_in(pe, u, 1)
                                diagonal_in(pe, 1, n)
                            if k >= s1_ring(u):
                                pe.wait_ge(max_done, k - s1_ring(u) + 1)
                            nc.tensor.matmul(s1[k % s1_ring(u)][:, :], st[:, u % 2, 0, g, (b - 1) * S:b * S],
                                             bd_slot(1, n)[:, g, :, :].rearrange("p j q -> p (j q)"),
                                             start=True, stop=True).then_inc(s1_full, 1)
                        if u >= 1 and b >= 1:
                            values(QB * (u - 1) + b - 1, g)
                        if u >= 1 and b >= 2 and g < 3:
                            (heads_by_query, heads_by_dim, project_out)[g](QB * (u - 1) + b - 2)
                        if (b, g) == (3, 3) and u + 1 < NQ:
                            transpose_context(u + 1)
                        if (b, g) == (4, 0) and u + 1 < NQ:
                            transpose_tokens(u + 1)
                        if (b, g) == (4, 0) and u + 1 == NQ:
                            fill(("x2T", 0))
                        if u == NQ:
                            for name in last_fills(NG * b + g):
                                fill(name)

            def down(n):
                q, k = divmod(n, NB)
                if k == 0:
                    if q >= 2:
                        pe.wait_ge(ysb_ready, q - 1)
                    if q == 0:
                        pe.wait_ge(x2_done, B)
                        for m in (3 * NB // 4 - 2, 3 * NB // 4 - 1):
                            taken(pe, ("W", m))
                pe.wait_ge(glo_ready, n + 1)
                for c, (w, g) in enumerate(((wt_hi, g_hi), (wt_hi, g_lo), (wt_lo, g_hi))):
                    last = nc.tensor.matmul(yb[q % 2][:, :], w[2][:, k, :], g[n % RH], start=(k == 0 and c == 0), stop=(k == NB - 1 and c == 2))
                last.then_inc(down_done, 1)

            for k in range(NB // 2 - 4, NB // 2):
                taken(pe, ("W", k))
            for n in range(NQ * NB):
                q, k = divmod(n, NB)
                if n < 2:
                    pe.wait_ge(prob_ready, NG * B)
                if n >= 2:
                    pe.wait_ge(sil_ready, n - 1)
                split_product(h1[n % 2][:, :], (wt_hi[0][:, k, :], wt_lo[0][:, k, :]), (x2_hi[q % 2], x2_lo[q % 2])).then_inc(h1_full, 1)
                if n >= 2:
                    pe.wait_ge(gg_ready, n - 1)
                split_product(h3[n % 2][:, :], (wt_hi[1][:, k, :], wt_lo[1][:, k, :]), (x2_hi[q % 2], x2_lo[q % 2])).then_inc(h3_full, 1)
                if n < 3:
                    (heads_by_query, heads_by_dim, project_out)[n](B - 1)
                if n >= LAG:
                    down(n - LAG)
                for name in unit_fills(n):
                    fill(name)
            for n in range(NQ * NB - LAG, NQ * NB):
                down(n)
            fill(("yT", NQ - 1))

        @block.scalar
        def _(act):
            def copy(o, i):
                return nc.scalar.activation(o, i, ACT.Copy)

            def full(name):
                act.wait_ge(work_full, slot[name] + 1)

            act.dma_start(cst[:, :], consts).then_inc(in_c, 16)
            act.dma_start(wg_nat[0:E, :], wg).then_inc(in_wg, 16)
            act.dma_start(ctx_all[:, 0:QB, :], ctx_d[0]).then_inc(in_ctx[0], 16)
            act.dma_start(w_nat[:, 3, :], Wo).then_inc(in_wo, 16)
            full("w")
            wb = work_bank("w")
            copy(w_hi[:, :, :].rearrange("p a d -> p (a d)"), wb[:, 0:2 * D]).then_inc(wT_hi_ready, 1)
            copy(wg_hi[:, :], wb[:, 3 * P:3 * P + E]).then_inc(wT_hi_ready, 1)
            act.wait_ge(wT_hi_ready, 2)
            act.wait_ge(ws_cleared, 1)
            copy(stack_columns(ws_hi), three_times(w_hi)).then_inc(ws_ready, 1)

            def take_heads(n):
                act.wait_ge(o_full, n + 1)
                if n >= 2:
                    act.wait_ge(oq_full, n - 1)
                copy(oT[:, n % 2, :], ob[n % 2][:, 0:2 * P]).then_inc(oT_ready, 1)

            def take_normalised(n):
                act.wait_ge(on_full, n + 1)
                if n:
                    act.wait_ge(y_full, n)
                copy(onT[:, :], ob[n % 2][:, 0:P]).then_inc(onT_ready, 1)

            def take_weights(k):
                full(("W", k))
                if k == NB // 2:
                    act.wait_ge(s2_full, NG * (B - 2))
                copy(wt_hi[k // 4][:, 4 * (k % 4):4 * (k % 4) + 4, :].rearrange("p k c -> p (k c)"),
                     work_bank(("W", k))[:, :]).then_inc(whi_ready, 1)

            def prepare(q):
                full(("x2T", q))
                if q >= 2:
                    act.wait_ge(h3_full, NB * (q - 1))
                copy(x2_hi[q % 2], work_bank(("x2T", q))[:, :]).then_inc(x2hi_ready, 1)

            def squash(q):
                act.wait_ge(dif_ready, q + 1)
                nc.scalar.activation(th[:, :, :], dif[:, :, :], ACT.Tanh, scale=0.5).then_inc(th_ready, 1)

            def next_tokens(u, step):
                if step == 0 and u < NQ:
                    full(("cT", u))
                    if u:
                        act.wait_ge(ck_ready, u)
                    copy(cT[:, :], work_bank(("cT", u))[:, :]).then_inc(into_sbuf(("cT", u)), 1)
                if step == 1 and u < NQ:
                    full(("xT", u))
                    copy(x_hi[:, :], work_bank(("xT", u))[:, :]).then_inc(xhi_ready, 1)
                if step == 1 and u == NQ:
                    prepare(0)
                if step == 3 and u < NQ:
                    act.wait_ge(ck_ready, u + 1)
                    copy(ck_hi[:, :], ck[:, :]).then_inc(ckhi_ready, 1)

            for g in range(NG):
                next_tokens(0, g)
            for u in range(NQ + 1):
                last_n = QB * (u - 1) - 1
                if u >= 2:
                    take_heads(last_n)
                if u < NQ:
                    full(("V", u))
                    if u >= 2:
                        act.wait_ge(o_full, QB * (u - 1))
                    src = work_bank(("V", u))[:, :].rearrange("p (m i j d) -> p m i j d", i=2, j=NJ, d=HD)
                    dst = va[u % 2].rearrange("p (m i j) r -> p m i j r", i=2, j=NJ)
                    if u < 2:
                        act.wait_ge(va_cleared, u + 1)
                    for i in range(2):
                        last = copy(dst[:, :, i, :, HD * i:HD * (i + 1)], src[:, :, i, :, :])
                    last.then_inc(into_sbuf(("V", u)), 1)
                    for k, (is_k, g) in enumerate(STACKS):
                        if k == 2 and u >= 2:
                            take_normalised(last_n)
                        n = NS * u + k
                        full(("st", u, k))
                        if k >= SH:
                            taken(act, ("st", u, k - SH))
                        elif u:
                            taken(act, ("st", u - 1, NS + k - SH))
                        src = work_bank(("st", u, k))[:, :]
                        if is_k:
                            i = copy(st_hi[:, n % SH, :], src)
                        else:
                            i = nc.scalar.activation(st_hi[:, n % SH, :], src, ACT.Identity, bias=cst[:, C_ONE:C_ONE + 1])
                        i.then_inc(sthi_ready, 1)
                if u == NQ:
                    take_normalised(last_n)
                for b in range(QB + 1 if u else 0):
                    for g in range(NG):
                        if b == QB and u < NQ:
                            next_tokens(u + 1, g)
                        if b >= 2 and g == 0:
                            take_heads(QB * (u - 1) + b - 2)
                        if b >= 2 and g == 2:
                            take_normalised(QB * (u - 1) + b - 2)
                        if u == NQ:
                            for name in last_fills(NG * b + g - 1):
                                if name[0] == "W":
                                    take_weights(name[1])
                                if name[0] == "x2T":
                                    prepare(1)
                            if (b, g) == (1, 2):
                                squash(0)
                        if b < QB:
                            n = QB * (u - 1) + b
                            k = NG * n + g
                            act.wait_ge(s2_full, k + 1)
                            if g == 0 and n >= 2:
                                act.wait_ge(o_full, n - 1)
                            nc.scalar.activation(prob[n % 2][:, NJ * g:NJ * (g + 1), :].rearrange("p h q -> p (h q)"),
                                                 s2[k % 2][:, :], ACT.Exp, scale=SCALE).then_inc(prob_ready, 1)
                if u == 0:
                    for g in range(NG):
                        next_tokens(1, g)

            def round_hidden(n):
                act.wait_ge(gg_ready, n + 1)
                if n >= RH:
                    act.wait_ge(down_done, n - RH + 1)
                copy(g_hi[n % RH], gg[n % 3]).then_inc(ghi_ready, 1)

            def take_y(q):
                act.wait_ge(down_done, NB * (q + 1))
                if q:
                    act.wait_ge(work_full, slot["yT", q - 1] + 1)
                copy(y_sb[:, :], yb[q % 2][:, :]).then_inc(ysb_ready, 1)

            take_heads(B - 1)
            nc.scalar.activation(unused[:, :], cst[:, C_ONE:C_ONE + 1], ACT.Silu)
            for n in range(NQ * NB):
                q, k = divmod(n, NB)
                act.wait_ge(h1_full, n + 1)
                if n >= 3:
                    act.wait_ge(silw_ready, n - 2)
                nc.scalar.activation(sil[n % 3], h1[n % 2][:, :], ACT.Silu).then_inc(sil_ready, 1)
                if n == 1:
                    take_normalised(B - 1)
                if n:
                    round_hidden(n - 1)
                if k == LAG - 1 and q:
                    take_y(q - 1)
                if k == 2 and 2 <= q + 1 < NQ:
                    prepare(q + 1)
                if k == 10 and q + 1 < NQ:
                    squash(q + 1)
            round_hidden(NQ * NB - 1)
            take_y(NQ - 1)

        @block.gpsimd
        def _(pool):
            steps = [0]

            def own(ins):
                steps[0] += 1
                ins.then_inc(pool_done, 1)
                pool.wait_ge(pool_done, steps[0])

            def load_mask(u):
                if u:
                    pool.wait_ge(mask_ready, u)
                pool.dma_start(mask_i[:, :], mask_d[u].partition_broadcast(P)).then_inc(in_mask[u], 16)

            load_mask(0)
            nc.gpsimd.memset(halves[:, :], -0.5)
            nc.gpsimd.memset(ws_hi[:, :, :, :].bitcast(F32), 0.0)
            nc.gpsimd.memset(ws_lo[:, :, :, :].bitcast(F32), 0.0).then_inc(ws_cleared, 1)

            def inverse_deviation(m):
                pool.wait_ge(var_ready, m + 1)
                own(nc.gpsimd.tensor_scalar(ve[:, :], mv[:, m, :, 1], EPS, None, ALU.add))
                nc.gpsimd.tensor_tensor(rstd[:, m, :], ve[:, :], halves[:, :], ALU.pow).then_inc(rstd_ready, 1)

            inverse_deviation(0)
            for k in (0, 1, 2):
                nc.gpsimd.memset(bd[:, k, :].bitcast(F32), 0.0).then_inc(bd_cleared, 1)

            def mask_context(u):
                taken(pool, ("cT", u))
                pool.wait_ge(mask_ready, u + 1)
                if u:
                    pool.wait_ge(cklo_ready, u)
                nc.gpsimd.tensor_tensor(ck[:, :], cT[:, :], keep[:, u % 2, :], ALU.mult).then_inc(ck_ready, 1)

            mask_context(0)
            load_mask(1)
            for k in (3, 4, 5):
                nc.gpsimd.memset(bd[:, k, :].bitcast(F32), 0.0).then_inc(bd_cleared, 1)
            for u in range(NQ + 1):
                if u:
                    taken(pool, ("MT", u - 1))
                    if u >= 2:
                        pool.wait_ge(s2_full, NG * QB * (u - 1))
                    for g in range(NG):
                        nc.gpsimd.tensor_tensor(m_bd[:, NJ * g:NJ * (g + 1), :], mT[:, :].unsqueeze(1).to_broadcast([P, NJ, P]),
                                                cst[:, C_HEAD + NJ * g:C_HEAD + NJ * (g + 1)].unsqueeze(2).to_broadcast([P, NJ, P]),
                                                ALU.mult).then_inc(mbd_ready, 1)
                if u + 1 < NQ:
                    inverse_deviation(u + 1)
                    mask_context(u + 1)
                    if u + 2 < NQ:
                        load_mask(u + 2)
                if u + 1 == NQ:
                    inverse_deviation(NQ)
            inverse_deviation(NQ + 1)
            inverse_deviation(NQ + 2)

            for n in range(NQ * NB):
                q, k = divmod(n, NB)
                pool.wait_ge(sil_ready, n + 1)
                if k % 2 == 0:
                    pool.wait_ge(in_ewb[k // 2], 16 * (q + 1))
                if n >= 3:
                    pool.wait_ge(gg_ready, n - 2)
                nc.gpsimd.tensor_tensor(silw[n % 3], sil[n % 3], ewb[:, k // 2, :], ALU.mult).then_inc(silw_ready, 1)
                if n == 5:
                    inverse_deviation(2 * NQ - 1)

        @block.vector
        def _(dve):
            steps = [0]

            def mark(ins):
                steps[0] += 1
                ins.then_inc(dve_done, 1)
                return steps[0]

            def own(ins):
                dve.wait_ge(dve_done, mark(ins))

            def full(name):
                dve.wait_ge(work_full, slot[name] + 1)

            marked = [0]

            def row_statistics(n0, b):
                marked[0] = mark(nc.vector.bn_stats(stats[:, b, :], x_all[:, n0 + b, :]))

            def mean_variance(m):
                dve.wait_ge(dve_done, marked[0])
                for b in range(QB):
                    ins = nc.vector.bn_aggr(mv[:, m, b, :], stats[:, b, :])
                    if b < QB - 1:
                        mark(ins)
                ins.then_inc(var_ready, 1)

            def statistics(n0, m):
                for b in range(QB):
                    row_statistics(n0, b)
                mean_variance(m)

            def normalise_batch(n0, m, b):
                if b == 0:
                    dve.wait_ge(rstd_ready, m + 1)
                nc.vector.tensor_scalar(xn[:, b, :], x_all[:, n0 + b, :], mv[:, m, b, 0:1], rstd[:, m, b:b + 1],
                                        ALU.subtract, ALU.mult).then_inc(xn_ready, 1)

            def normalise(n0, m):
                for b in range(QB):
                    normalise_batch(n0, m, b)

            def masks(u, step):
                if step == 0:
                    dve.wait_ge(in_mask[u], 16)
                    if u >= 2:
                        dve.wait_ge(work_full, slot["st", u - 2, NS - 1] + 1)
                        dve.wait_ge(ck_ready, u - 1)
                    marked[0] = mark(nc.vector.tensor_scalar(nokeep[:, u % 2, :], mask_i[:, :], 0, None, ALU.is_equal))
                else:
                    dve.wait_ge(dve_done, marked[0])
                    nc.vector.tensor_scalar(keep[:, u % 2, :], nokeep[:, u % 2, :].bitcast(F32), -1.0, 1.0, ALU.mult, ALU.add
                                            ).then_inc(mask_ready, 1)

            def clear_values(k):
                own(nc.vector.memset(va[k][:, :, :], 0.0))
                v = va[k].rearrange("p (m i j) r -> p m i j r", i=2, j=NJ)
                nc.vector.memset(v[:, :, 0, :, 16:17], 1.0)
                nc.vector.memset(v[:, :, 1, :, 17:18], 1.0).then_inc(va_cleared, 1)

            clear_values(0)
            dve.wait_ge(in_x[0], 16)
            statistics(0, 0)
            full("w")
            wb = work_bank("w")
            dve.wait_ge(wT_hi_ready, 2)
            nc.vector.tensor_copy(wvT[:, :], wb[:, 2 * P:3 * P]).then_inc(setup_ready, 1)
            nc.vector.tensor_tensor(wg_lo[:, :], wb[:, 3 * P:3 * P + E], wg_hi[:, :].bitcast(F32), ALU.subtract)
            nc.vector.tensor_tensor(w_lo[:, :, :].rearrange("p a d -> p (a d)"), wb[:, 0:2 * D],
                                    w_hi[:, :, :].rearrange("p a d -> p (a d)").bitcast(F32), ALU.subtract).then_inc(into_sbuf("w"), 1)
            normalise(0, 0)
            taken(dve, "w")
            dve.wait_ge(ws_cleared, 1)
            nc.vector.tensor_copy(stack_columns(ws_lo), three_times(w_lo)).then_inc(ws_ready, 1)
            masks(0, 0)
            masks(0, 1)
            nc.vector.tensor_copy(bias_w[:, :], cst[:, C_BIAS:C_BIAS + P])
            nc.vector.tensor_copy(ones_b[:, :, :], cst[:, C_BATCH:C_BATCH + QB].unsqueeze(2).to_broadcast([P, QB, P])
                                  ).then_inc(setup_ready, 1)

            def take_projection(n):
                dve.wait_ge(y_full, n + 1)
                nc.vector.tensor_tensor(x_all[:, n, :], ob[n % 2][:, P:2 * P], x_all[:, n, :], ALU.add).then_inc(x2_done, 1)

            def normalise_heads(n):
                dve.wait_ge(oq_full, n + 1)
                heads = ob[n % 2][:, 2 * P:4 * P].rearrange("p (m r) -> p m r", r=R)
                own(nc.vector.reciprocal(rz[:, :].rearrange("p (m i) -> p m i", i=2), heads[:, :, 16:18]))
                if n:
                    dve.wait_ge(on_full, n)
                nc.vector.tensor_tensor(on[:, :].rearrange("p (m i d) -> p m i d", i=2, d=HD),
                                        heads[:, :, 0:16].rearrange("p m (i d) -> p m i d", i=2),
                                        rz[:, :].rearrange("p (m i) -> p m i", i=2).unsqueeze(3).to_broadcast([P, 8, 2, HD]),
                                        ALU.mult).then_inc(on_ready, 1)

            def round_maxima():
                own(nc.vector.tensor_copy(m_hi[:, :], m_neg[:, :]))
                nc.vector.tensor_copy(m_hl[:, 0, :], m_hi[:, :].bitcast(F32))
                nc.vector.tensor_tensor(m_hl[:, 1, :], m_neg[:, :], m_hi[:, :].bitcast(F32), ALU.subtract).then_inc(mhl_ready, 1)

            def second_statistics(q):
                dve.wait_ge(x2_done, QB * (q + 1))
                statistics(QB * q, NQ + q)

            def split_x2(q):
                full(("x2T", q))
                dve.wait_ge(x2hi_ready, q + 1)
                if q >= 2:
                    dve.wait_ge(h3_full, NB * (q - 1))
                nc.vector.tensor_tensor(x2_lo[q % 2], work_bank(("x2T", q))[:, :], x2_hi[q % 2].bitcast(F32),
                                        ALU.subtract).then_inc(into_sbuf(("x2T", q)), 1)

            def routing_step(q, k):
                other = lg[:, :, :].unsqueeze(2).to_broadcast([P, QB, E, E])
                this = lg[:, :, :].unsqueeze(3).to_broadcast([P, QB, E, E])
                lower = cst[:, C_LOW:C_LOW + E * E].rearrange("p (e f) -> p e f", e=E)
                if k == 0:
                    full(("lg", q))
                    nc.vector.tensor_copy(lg[:, :, :].rearrange("p b e -> p (b e)"),
                                          work_bank(("lg", q))[:, 0:QB * E]).then_inc(into_sbuf(("lg", q)), 1)
                    taken(dve, ("lg", q))
                if k < 2:
                    for b in (2 * k, 2 * k + 1):
                        own(nc.vector.tensor_tensor(eq[:, b], other[:, b], this[:, b], ALU.is_equal))
                        nc.vector.tensor_tensor(gt[:, b], other[:, b], this[:, b], ALU.is_gt)
                        last = mark(nc.vector.tensor_tensor(eq[:, b], eq[:, b], lower, ALU.mult))
                    dve.wait_ge(dve_done, last)
                if k == 2:
                    own(nc.vector.tensor_tensor(gt, gt, eq, ALU.add))
                    own(nc.vector.tensor_reduce(rank[:, :, :], gt, X, ALU.add))
                if k == 3:
                    own(nc.vector.tensor_scalar(sel[:, :, :], rank[:, :, :], 2.0, None, ALU.is_lt))
                    own(nc.vector.tensor_tensor(ew[:, :, :], sel[:, :, :], lg[:, :, :], ALU.mult))
                    own(nc.vector.tensor_reduce(lsum[:, :], ew[:, :, :], X, ALU.add))
                    nc.vector.scalar_tensor_tensor(dif[:, :, :], lg[:, :, :], 2.0, lsum[:, :].unsqueeze(2).to_broadcast([P, QB, E]),
                                                   ALU.mult, ALU.subtract).then_inc(dif_ready, 1)
                if k == 4:
                    dve.wait_ge(th_ready, q + 1)
                    own(nc.vector.tensor_scalar(ew[:, :, :], th[:, :, :], 0.5, 0.5, ALU.mult, ALU.add))
                    nc.vector.tensor_tensor(ew[:, :, :], ew[:, :, :], sel[:, :, :], ALU.mult).then_inc(ew_ready, 1)

            def take_weights(q):
                full(("ewT", q))
                if q:
                    for e in range(E):
                        dve.wait_ge(in_ewb[e], 16 * q)
                nc.vector.tensor_copy(ewT, work_bank(("ewT", q))[0:E, :]).then_inc(into_sbuf(("ewT", q)), 1)

            def finish(q):
                full(("yT", q))
                if q:
                    dve.wait_ge(out_done, 16 * q)
                nc.vector.tensor_tensor(o_sb.rearrange("p b d -> p (b d)"), work_bank(("yT", q))[:, :],
                                        x_all[:, QB * q:QB * (q + 1), :].rearrange("p b d -> p (b d)"),
                                        ALU.add).then_inc(into_sbuf(("yT", q)), 1)

            def rest_of_weights(k):
                full(("W", k))
                dve.wait_ge(whi_ready, k + 1)
                if k == NB // 2:
                    dve.wait_ge(s2_full, NG * (B - 1))
                piece = slice(4 * (k % 4), 4 * (k % 4) + 4)
                nc.vector.tensor_tensor(wt_lo[k // 4][:, piece, :].rearrange("p k c -> p (k c)"), work_bank(("W", k))[:, :],
                                        wt_hi[k // 4][:, piece, :].rearrange("p k c -> p (k c)").bitcast(F32),
                                        ALU.subtract).then_inc(into_sbuf(("W", k)), 1)

            def split_tokens(u):
                full(("xT", u))
                dve.wait_ge(xhi_ready, u + 1)
                nc.vector.tensor_tensor(x_lo[:, :], work_bank(("xT", u))[:, :], x_hi[:, :].bitcast(F32),
                                        ALU.subtract).then_inc(into_sbuf(("xT", u)), 1)

            split_tokens(0)
            for u in range(NQ + 1):
                if u >= 2:
                    normalise_heads(QB * (u - 1) - 1)
                if u >= 1:
                    full(("MT", u - 1))
                    if u >= 2:
                        dve.wait_ge(mbd_ready, NG * (u - 1))
                    nc.vector.tensor_copy(mT[:, :], work_bank(("MT", u - 1))[:, 0:P]).then_inc(into_sbuf(("MT", u - 1)), 1)
                if u == NQ:
                    take_projection(QB * (u - 1) - 1)
                if u == 0:
                    dve.wait_ge(in_wo, 16)
                    for half in range(2):
                        cols = slice(half * D // 2, (half + 1) * D // 2)
                        last = nc.vector.tensor_copy(wo_p[:, cols].rearrange("p (j i d) -> p j i d", i=2, d=HD),
                                                     w_nat[:, 3, cols].rearrange("p (i j d) -> p j i d", i=2, d=HD))
                    last.then_inc(wo_p_ready, 1)
                if u < NQ:
                    dve.wait_ge(ckhi_ready, u + 1)
                    nc.vector.tensor_tensor(ck_lo[:, :], ck[:, :], ck_hi[:, :].bitcast(F32), ALU.subtract).then_inc(cklo_ready, 1)
                    if u >= 2:
                        dve.wait_ge(s1_full, NG * QB * (u - 1))
                        dve.wait_ge(s2_full, NG * QB * (u - 1))
                        for n in range(QB * (u - 1) - 3, QB * (u - 1)):
                            diagonal_in(dve, 1, n)
                            diagonal_in(dve, 0, n)
                    for k, (is_k, g) in enumerate(STACKS):
                        if k == 4 and u >= 2:
                            take_projection(QB * (u - 1) - 1)
                        n = NS * u + k
                        full(("st", u, k))
                        dve.wait_ge(sthi_ready, n + 1)
                        nc.vector.scalar_tensor_tensor(
                            st[:, u % 2, is_k, g, :], st_hi[:, n % SH, :].bitcast(F32),
                            cst[:, (C_CK if is_k else C_CQ):(C_CK if is_k else C_CQ) + 1],
                            work_bank(("st", u, k))[:, :], ALU.mult, ALU.add).then_inc(into_sbuf(("st", u, k)), 1)
                if u == 0:
                    full("wo")
                    nc.vector.tensor_copy(wo_s[:, :], work_bank("wo")[:, 0:D]).then_inc(into_sbuf("wo"), 1)
                    clear_values(1)
                for b in range(QB + 1):
                    for g in range(NG):
                        if u < NQ:
                            n0, m = (QB * (u + 1), u + 1) if u + 1 < NQ else (0, NQ)
                            if (b, g) == (1, 0):
                                if u + 1 < NQ:
                                    dve.wait_ge(in_x[u + 1], 16)
                                else:
                                    dve.wait_ge(x2_done, QB)
                            if b == 1:
                                row_statistics(n0, g)
                            if (b, g) == (2, 0):
                                mean_variance(m)
                            if b == 2 and g in (1, 2) and u + 1 < NQ:
                                masks(u + 1, g - 1)
                            if b == 3:
                                normalise_batch(n0, m, g)
                            if (b, g) == (4, 2):
                                if u + 1 < NQ:
                                    split_tokens(u + 1)
                                else:
                                    split_x2(0)
                        if u >= 1 and b >= 2 and g == 1:
                            normalise_heads(QB * (u - 1) + b - 2)
                        if u >= 1 and b >= 2 and g == 3:
                            take_projection(QB * (u - 1) + b - 2)
                        if u == NQ:
                            tick = NG * b + g
                            for name in last_fills(tick - 1):
                                if name[0] == "W":
                                    rest_of_weights(name[1])
                                if name[0] == "lg":
                                    routing_step(0, 0)
                                if name[0] == "x2T":
                                    split_x2(1)
                            if tick == 6:
                                second_statistics(1)
                            if tick == 9:
                                normalise(QB, NQ + 1)
                            if tick == 11:
                                second_statistics(2)
                            if 1 <= tick < 4:
                                routing_step(0, tick)
                            if tick == 7:
                                routing_step(0, 4)
                            if tick == 9:
                                take_weights(0)
                        if u < NQ and b >= 1:
                            k = NG * (QB * u + b - 1) + g
                            dve.wait_ge(s1_full, k + 1)
                            nc.vector.tensor_reduce(m_neg[:, H * (b - 1) + NJ * g:H * (b - 1) + NJ * (g + 1)],
                                                    s1[k % s1_ring(u)][:, :].rearrange("p (j q) -> p j q", j=NJ), X, ALU.max,
                                                    negate=True).then_inc(max_done, 1)
                    if u < NQ and b == QB:
                        dve.wait_ge(max_done, NG * QB * (u + 1))
                        round_maxima()
            def hidden_rest(n):
                dve.wait_ge(ghi_ready, n + 1)
                dve.wait_ge(gg_ready, n + 1)
                if n >= RH:
                    dve.wait_ge(down_done, n - RH + 1)
                nc.vector.tensor_tensor(g_lo[n % RH], gg[n % 3], g_hi[n % RH].bitcast(F32), ALU.subtract).then_inc(glo_ready, 1)

            for n in range(NQ * NB):
                q, k = divmod(n, NB)
                if n == 0:
                    normalise_heads(B - 1)
                if n == 3:
                    take_projection(B - 1)
                dve.wait_ge(silw_ready, n + 1)
                dve.wait_ge(h3_full, n + 1)
                if n >= 3:
                    dve.wait_ge(glo_ready, n - 2)
                nc.vector.tensor_tensor(gg[n % 3], silw[n % 3], h3[n % 2][:, :], ALU.mult).then_inc(gg_ready, 1)
                if n:
                    hidden_rest(n - 1)
                if k == LAG + 3 and q:
                    finish(q - 1)
                if n == 4:
                    second_statistics(NQ - 1)
                if 2 <= q + 1 < NQ:
                    if k == 2:
                        split_x2(q + 1)
                if q + 2 < NQ and k == 14:
                    normalise(QB * (q + 2), NQ + q + 2)
                if q + 1 < NQ:
                    if 5 <= k < 9:
                        routing_step(q + 1, k - 5)
                    if k == 10:
                        routing_step(q + 1, 4)
                    if k == 12:
                        take_weights(q + 1)
            hidden_rest(NQ * NB - 1)
            finish(NQ - 1)


_INS = ["x", "ctx_1024", "mask_BxS2_if1", "L0_xattn_Wq", "L0_xattn_Wk", "L0_xattn_Wv", "L0_xattn_Wo", "L0_ffn_wg",
        "L0_ffn_w1", "L0_ffn_w3", "L0_ffn_w2"]


def kernel(**inputs):
    import concourse.bacc as bacc
    from concourse.bass_utils import run_bass_kernel_spmd

    nc = bacc.Bacc("TRN2", target_bir_lowering=False, num_devices=1)
    arrays = {f"in_{name}": np.ascontiguousarray(inputs[name]) for name in _INS}
    arrays["in_patterns"] = constants()
    args = [nc.dram_tensor(name, a.shape, mybir.dt.from_np(a.dtype), kind="ExternalInput").ap() for name, a in arrays.items()]
    out = nc.dram_tensor("out", (B, S, D), F32, kind="ExternalOutput").ap()
    ew_rows = nc.dram_tensor("ew_rows", (NQ, E, T), F32, kind="Internal").ap()
    program(nc, *args, ew_rows, out)
    return run_bass_kernel_spmd(nc, [arrays], core_ids=[0]).results[0]["out"]
```
